# Optimizing a Trainium2 kernel written in Bass

```python
import numpy as np
import jax
import jax.numpy as jnp

def _softmax(x, axis=-1):
    return jax.nn.softmax(x, axis=axis)
def _gelu(x):
    return jax.nn.gelu(x, approximate=True)
def _silu(x):
    return jax.nn.silu(x)
def _sigmoid(x):
    return jax.nn.sigmoid(x)
def _layernorm(x, axis=-1, eps=1e-5):
    m = jnp.mean(x, axis=axis, keepdims=True)
    v = jnp.var(x, axis=axis, keepdims=True)
    return (x - m) / jnp.sqrt(v + eps)
def _scatter_add(tgt, idx, src, axis=0):
    return tgt.at[idx].add(src)
def _segment_sum(src, seg, n):
    return jax.ops.segment_sum(src, seg, n)

kernel_name = 'mk_adj_seq_d1_adj_512_49997e'

def setup_inputs(seed: int = 0):
    np.random.seed(seed)
    _w = jnp.asarray
    def _rec_inputs():
        import jax
        import jax.numpy as jnp
        _gk = jax.random.key(seed)
        x = -0.0005207 + 1.001 * jax.random.normal(jax.random.fold_in(_gk, 1), (4096, 512), jnp.float32)
        _w = (1.0 + jnp.arange(4096, dtype=jnp.float32)) ** -0.5
        _w = _w / _w.mean()
        _pij = jnp.clip(0.00195312 * _w[:, None] * _w[None, :], 0.0, 1.0)
        _a = jax.random.uniform(jax.random.fold_in(_gk, 2), (4096, 4096)) < _pij
        adj = _a.astype(jnp.int32)
        return x, adj
    x, adj = _rec_inputs()
    def _L0_gnn_setup():
        import jax, jax.numpy as jnp
        import numpy as np
        D_MODEL = 512
        N_HEADS = 8
        D_K = D_MODEL // N_HEADS
        D_FF = 2048
        N = 4096
        EPS = 1e-05

        def _layer_norm(x, g, b):
            mu = jnp.mean(x, axis=-1, keepdims=True)
            var = jnp.mean(jnp.square(x - mu), axis=-1, keepdims=True)
            return (x - mu) * jax.lax.rsqrt(var + EPS) * g + b
        key = jax.random.key(seed)
        ks = jax.random.split(key, 16)
        s = 1.0 / np.sqrt(D_MODEL)
        sf = 1.0 / np.sqrt(D_FF)
        inp = {'h': jax.random.normal(ks[0], (N, D_MODEL), dtype=jnp.float32), 'adj': jax.random.randint(ks[1], (N, N), 0, 2, dtype=jnp.int32), 'Wq': jax.random.uniform(ks[2], (D_MODEL, D_MODEL), jnp.float32, -s, s), 'bq': jnp.zeros((D_MODEL,), jnp.float32), 'Wk': jax.random.uniform(ks[3], (D_MODEL, D_MODEL), jnp.float32, -s, s), 'bk': jnp.zeros((D_MODEL,), jnp.float32), 'Wv': jax.random.uniform(ks[4], (D_MODEL, D_MODEL), jnp.float32, -s, s), 'bv': jnp.zeros((D_MODEL,), jnp.float32), 'Wo': jax.random.uniform(ks[5], (D_MODEL, D_MODEL), jnp.float32, -s, s), 'bo': jnp.zeros((D_MODEL,), jnp.float32), 'W1': jax.random.uniform(ks[6], (D_FF, D_MODEL), jnp.float32, -s, s), 'b1': jnp.zeros((D_FF,), jnp.float32), 'W2': jax.random.uniform(ks[7], (D_MODEL, D_FF), jnp.float32, -sf, sf), 'b2': jnp.zeros((D_MODEL,), jnp.float32), 'ln1_g': jnp.ones((D_MODEL,), jnp.float32), 'ln1_b': jnp.zeros((D_MODEL,), jnp.float32), 'ln2_g': jnp.ones((D_MODEL,), jnp.float32), 'ln2_b': jnp.zeros((D_MODEL,), jnp.float32)}
        return inp
    _L0_gnn_all = _L0_gnn_setup()
    _L0_gnn_in = {k: v for k, v in _L0_gnn_all.items() if k in ('Wq', 'bq', 'Wk', 'bk', 'Wv', 'bv', 'Wo', 'bo', 'W1', 'b1', 'W2', 'b2', 'ln1_g', 'ln1_b', 'ln2_g', 'ln2_b', )}
    del _L0_gnn_all

    return {
        "x": x,
        "adj": adj,
        "L0_gnn_Wq": _L0_gnn_in["Wq"],
        "L0_gnn_bq": _L0_gnn_in["bq"],
        "L0_gnn_Wk": _L0_gnn_in["Wk"],
        "L0_gnn_bk": _L0_gnn_in["bk"],
        "L0_gnn_Wv": _L0_gnn_in["Wv"],
        "L0_gnn_bv": _L0_gnn_in["bv"],
        "L0_gnn_Wo": _L0_gnn_in["Wo"],
        "L0_gnn_bo": _L0_gnn_in["bo"],
        "L0_gnn_W1": _L0_gnn_in["W1"],
        "L0_gnn_b1": _L0_gnn_in["b1"],
        "L0_gnn_W2": _L0_gnn_in["W2"],
        "L0_gnn_b2": _L0_gnn_in["b2"],
        "L0_gnn_ln1_g": _L0_gnn_in["ln1_g"],
        "L0_gnn_ln1_b": _L0_gnn_in["ln1_b"],
        "L0_gnn_ln2_g": _L0_gnn_in["ln2_g"],
        "L0_gnn_ln2_b": _L0_gnn_in["ln2_b"],
    }

def reference(x, adj, L0_gnn_Wq, L0_gnn_bq, L0_gnn_Wk, L0_gnn_bk, L0_gnn_Wv, L0_gnn_bv, L0_gnn_Wo, L0_gnn_bo, L0_gnn_W1, L0_gnn_b1, L0_gnn_W2, L0_gnn_b2, L0_gnn_ln1_g, L0_gnn_ln1_b, L0_gnn_ln2_g, L0_gnn_ln2_b):
    import jax
    import jax.numpy as jnp
    def _L0_gnn_ref(h, adj, Wq, bq, Wk, bk, Wv, bv, Wo, bo, W1, b1, W2, b2, ln1_g, ln1_b, ln2_g, ln2_b):
        import jax, jax.numpy as jnp
        import numpy as np
        D_MODEL = 512
        N_HEADS = 8
        D_K = D_MODEL // N_HEADS
        D_FF = 2048
        N = 4096
        EPS = 1e-05

        def _layer_norm(x, g, b):
            mu = jnp.mean(x, axis=-1, keepdims=True)
            var = jnp.mean(jnp.square(x - mu), axis=-1, keepdims=True)
            return (x - mu) * jax.lax.rsqrt(var + EPS) * g + b
        n = h.shape[0]
        mask = adj.astype(jnp.float32) + jnp.eye(n, dtype=jnp.float32)
        q = (h @ Wq.T + bq).reshape(n, N_HEADS, D_K)
        k = (h @ Wk.T + bk).reshape(n, N_HEADS, D_K)
        v = (h @ Wv.T + bv).reshape(n, N_HEADS, D_K)
        scores = jnp.einsum('nhd,mhd->hnm', q, k) / jnp.sqrt(jnp.float32(D_K))
        scores = jnp.where(mask[None, :, :] == 0, jnp.float32(-1000000000.0), scores)
        attn = jax.nn.softmax(scores, axis=-1)
        ctx = jnp.einsum('hnm,mhd->nhd', attn, v).reshape(n, D_MODEL)
        attn_out = ctx @ Wo.T + bo
        h1 = _layer_norm(h + attn_out, ln1_g, ln1_b)
        ff = jax.nn.relu(h1 @ W1.T + b1) @ W2.T + b2
        h2 = _layer_norm(h1 + ff, ln2_g, ln2_b)
        return h2

    x = _L0_gnn_ref(x, adj, L0_gnn_Wq, L0_gnn_bq, L0_gnn_Wk, L0_gnn_bk, L0_gnn_Wv, L0_gnn_bv, L0_gnn_Wo, L0_gnn_bo, L0_gnn_W1, L0_gnn_b1, L0_gnn_W2, L0_gnn_b2, L0_gnn_ln1_g, L0_gnn_ln1_b, L0_gnn_ln2_g, L0_gnn_ln2_b)
    return x


_drawn_inputs = setup_inputs


def setup_inputs(seed=0):
    import zlib

    import numpy as np

    out = dict(_drawn_inputs(seed))
    spreads = {'L0_gnn_bq': (0.0, 0.8),
     'L0_gnn_bk': (0.0, 0.8),
     'L0_gnn_bv': (0.0, 0.1),
     'L0_gnn_bo': (0.0, 0.1),
     'L0_gnn_b1': (0.0, 0.1),
     'L0_gnn_b2': (0.0, 0.1),
     'L0_gnn_ln1_g': (1.0, 0.2),
     'L0_gnn_ln1_b': (0.0, 0.1),
     'L0_gnn_ln2_g': (1.0, 0.2),
     'L0_gnn_ln2_b': (0.0, 0.1)}
    factors = {}
    for name, (base, spread) in spreads.items():
        noise = np.random.default_rng([zlib.crc32(name.encode()), seed]).standard_normal(out[name].shape)
        drawn = base * np.exp(spread * noise) if base else spread * noise
        out[name] = jnp.asarray(drawn.astype(out[name].dtype))
    for name, factor in factors.items():
        out[name] = (out[name] * factor).astype(out[name].dtype)
    return out
```

```python
import numpy as np
import concourse.bass as bass
from concourse import mybir
from contextlib import ExitStack

F32 = mybir.dt.float32
I32 = mybir.dt.int32
U32 = mybir.dt.uint32
ALU = mybir.AluOpType
ACT = mybir.ActivationFunctionType
AX = mybir.AxisListType

P = 128
N = 4096
D = 512
H = 8
DK = D // H
F = 2048
EPS = 1e-5
SCALE = DK ** -0.5
CD = D // P
CF = F // P
T = N // P
G = 512
NG = N // G
TG = G // P
CK = 4
KEYS = CK * P
MASKED = -8e9
RESET = 1e30
ITEMS = T * (N // KEYS)
TAB_K, TAB_ADJ, TAB_REL, TAB_Q, TAB_V, TAB_KEEP, TAB_RST, TAB_OUT, TAB = 0, 4, 8, 12, 13, 17, 18, 19, 21
AHEAD = 3


def wait_alone(engine, passed, *waits):
    for semaphore, value in waits:
        engine.wait_ge(semaphore, value)
        engine.sem_inc(passed, 1)


def project_qkv(nc, xT, wT, b_q, b_k, b_v, q_tab, kv_tab):
    with ExitStack() as ctx:
        sb = lambda name, shape, dt=F32: ctx.enter_context(nc.sbuf_tensor(f"qkv_{name}", shape, dt))
        sem = lambda name: ctx.enter_context(nc.semaphore(f"qkv_{name}"))
        w = [sb(f"w_{n}", [P, CD, D]) for n in "qkv"]
        bq = sb("bq", [P, CD])
        bkv = sb("bkv", [P, 2, D])
        x = [sb(f"x_{b}", [P, CD, G]) for b in range(2)]
        q = [sb(f"q_{b}", [P, TG, CD, P]) for b in range(2)]
        kv = [sb(f"kv_{b}", [P, TG, 2, D]) for b in range(2)]
        q_ps = ctx.enter_context(nc.psum_tensor("qkv_q_ps", [P, 4, G], F32))
        kv_ps = ctx.enter_context(nc.psum_tensor("qkv_kv_ps", [P, 4, D], F32))
        w_in = sem("w_in")
        x_in = [sem(f"x_in_{b}") for b in range(2)]
        q_out = [sem(f"q_out_{b}") for b in range(2)]
        kv_out = [sem(f"kv_out_{b}") for b in range(2)]
        q_sum, q_done = sem("q_sum"), sem("q_done")
        kv_sum, kv_done = sem("kv_sum"), sem("kv_done")
        passed = sem("passed")
        block = ctx.enter_context(nc.Block())

        @block.sync
        def _(sp):
            for n in range(3):
                sp.dma_start(w[n][:, :, :], wT[n].rearrange("(c p) o -> p c o", p=P)).then_inc(w_in, 16)
            sp.dma_start(bq[:, :], b_q).then_inc(w_in, 16)
            for n, b in enumerate((b_k, b_v)):
                sp.dma_start(bkv[:, n, :], b.rearrange("(a o) -> a o", a=1).broadcast_to([P, D])).then_inc(w_in, 16)

            def load(g, b):
                sp.dma_start(x[b][:, :, :], xT[:, bass.ds(g * G, G)].rearrange("(c p) n -> p c n", p=P)).then_inc(x_in[b], 16)

            def store(g, b):
                wait_alone(sp, passed, (q_done, (g + 1) * CD))
                sp.dma_start(q_tab[bass.ds(g * G, G), :].rearrange("(t p) f -> p t f", p=P),
                             q[b][:, :, :, :].rearrange("p t c q -> p t (c q)")).then_inc(q_out[b], 16)
                wait_alone(sp, passed, (kv_done, (g + 1) * 2 * TG))
                for n in range(2):
                    sp.dma_start(kv_tab[n][bass.ds(g * G, G), :].rearrange("(t p) f -> p t f", p=P),
                                 kv[b][:, :, n, :]).then_inc(kv_out[b], 16)

            load(0, 0)
            load(1, 1)
            with sp.Fori(0, NG // 2 - 1) as pair:
                g2 = pair * 2
                for b in range(2):
                    store(g2 + b, b)
                    load(g2 + b + 2, b)
            for b in range(2):
                store(NG - 2 + b, b)
            for b in range(2):
                sp.wait_ge(q_out[b], 16 * NG // 2)
                sp.wait_ge(kv_out[b], 16 * NG)

        @block.tensor
        def _(pe):
            pe.wait_ge(w_in, 16 * 6)

            def group(g, b, half):
                pe.wait_ge(x_in[b], half)
                for c in range(CD):
                    if not (isinstance(g, int) and g == 0):
                        pe.wait_ge(q_done, g * CD + c - 3)
                    for i in range(CD):
                        mm = pe.matmul(q_ps[:, c, :], w[0][:, i, c * P:(c + 1) * P], x[b][:, i, :],
                                       start=i == 0, stop=i == CD - 1)
                    mm.then_inc(q_sum, 1)
                for t in range(TG):
                    for n in range(2):
                        at = 2 * t + n
                        if at >= 4 or not (isinstance(g, int) and g == 0):
                            pe.wait_ge(kv_done, g * 2 * TG + at - 3)
                        for i in range(CD):
                            mm = pe.matmul(kv_ps[:, at % 4, :], x[b][:, i, t * P:(t + 1) * P], w[1 + n][:, i, :],
                                           start=i == 0, stop=i == CD - 1)
                        mm.then_inc(kv_sum, 1)

            for b in range(2):
                group(b, b, 16)
            with pe.Fori(1, NG // 2) as pair:
                g2 = pair * 2
                for b in range(2):
                    group(g2 + b, b, g2 * 8 + 16)

        @block.scalar
        def _(act):
            act.wait_ge(w_in, 16 * 6)

            def group(g, b, stored):
                if stored is not None:
                    act.wait_ge(q_out[b], stored)
                for c in range(CD):
                    act.wait_ge(q_sum, g * CD + c + 1)
                    act.activation(q[b][:, :, c, :], q_ps[:, c, :].rearrange("p (t q) -> p t q", q=P),
                                   ACT.Identity, bias=bq[:, c:c + 1]).then_inc(q_done, 1)

            for b in range(2):
                group(b, b, None)
            with act.Fori(1, NG // 2) as pair:
                g2 = pair * 2
                for b in range(2):
                    group(g2 + b, b, g2 * 8)

        @block.vector
        def _(dve):
            dve.wait_ge(w_in, 16 * 6)

            def group(g, b, stored):
                if stored is not None:
                    dve.wait_ge(kv_out[b], stored)
                for at in range(2 * TG):
                    dve.wait_ge(kv_sum, g * 2 * TG + at + 1)
                    dve.tensor_tensor(kv[b][:, at // 2, at % 2, :], kv_ps[:, at % 4, :], bkv[:, at % 2, :],
                                      ALU.add).then_inc(kv_done, 1)

            for b in range(2):
                group(b, b, None)
            with dve.Fori(1, NG // 2) as pair:
                g2 = pair * 2
                for b in range(2):
                    group(g2 + b, b, g2 * 16)


def attend(nc, tab, adj_tab, q_tab, k_tab, v_tab, ctx_out, ident_in, iota_in, items):
    with ExitStack() as ctx:
        sb = lambda name, shape, dt=F32: ctx.enter_context(nc.sbuf_tensor(f"att_{name}", shape, dt))
        two = lambda name, shape, dt=F32: [sb(f"{name}_{b}", shape, dt) for b in range(2)]
        ps = lambda name, shape: ctx.enter_context(nc.psum_tensor(f"att_{name}", shape, F32))
        sem = lambda name: ctx.enter_context(nc.semaphore(f"att_{name}"))
        ident = sb("ident", [P, P])
        iota = sb("iota", [P, P])
        tab_a = two("tab_a", [P, TAB_V], I32)
        tab_b = two("tab_b", [P, TAB_OUT - TAB_V], I32)
        tab_c = two("tab_c", [P, 2], I32)
        k = two("k", [P, CK, D])
        v = two("v", [P, CK, D])
        adj = two("adj", [P, CK, P], I32)
        qT = two("qT", [P, CD, P])
        maskT = two("maskT", [P, CK, P])
        mask = two("mask", [P, KEYS])
        kT = two("kT", [P, CD, KEYS])
        s = two("s", [P, H, KEYS])
        NPT = 3
        pT = sb("pT", [P, NPT, CK, P])
        gmax = two("gmax", [P, H])
        mold = sb("mold", [P, H])
        mrun = sb("mrun", [P, H])
        mdiff = two("mdiff", [P, H])
        negm = two("negm", [P, H])
        alpha = two("alpha", [P, H])
        gsum = two("gsum", [P, H])
        lrun = sb("lrun", [P, H])
        rinv = sb("rinv", [P, H])
        orun = sb("orun", [P, H, DK])
        cout = two("cout", [P, D])
        tr_ps = ps("tr_ps", [P, 2, KEYS])
        s_ps = ps("s_ps", [P, 2, KEYS])
        pT_ps = ps("pT_ps", [P, 2, KEYS])
        o_ps = ps("o_ps", [P, 2, D])
        const_in = sem("const_in")
        tab_a_in = [sem(f"tab_a_in_{b}") for b in range(2)]
        tab_b_in = [sem(f"tab_b_in_{b}") for b in range(2)]
        tab_c_in = [sem(f"tab_c_in_{b}") for b in range(2)]
        k_in = [sem(f"k_in_{b}") for b in range(2)]
        v_in = [sem(f"v_in_{b}") for b in range(2)]
        adj_in = [sem(f"adj_in_{b}") for b in range(2)]
        q_in = [sem(f"q_in_{b}") for b in range(2)]
        ctx_stored = sem("ctx_stored")
        maskT_done = sem("maskT_done")
        tr_done = sem("tr_done")
        tr_read = sem("tr_read")
        s_done = sem("s_done")
        s_read = sem("s_read")
        stat_done = sem("stat_done")
        alpha_done = sem("alpha_done")
        p_done = sem("p_done")
        pT_done = sem("pT_done")
        pT_read = sem("pT_read")
        pv_done = sem("pv_done")
        o_done = sem("o_done")
        c_done = sem("c_done")
        init = sem("init")
        chain = sem("chain")
        passed = sem("passed")
        block = ctx.enter_context(nc.Block())

        def known(i, least):
            return isinstance(i, int) and i < least

        def uses(i, b):
            return 16 * (i // 2 + 1) if isinstance(i, int) else (i - b) * 8 + 16

        @block.sync
        def _(sp):
            sp.dma_start(ident[:, :], ident_in).then_inc(const_in, 16)
            sp.dma_start(iota[:, :], iota_in).then_inc(const_in, 16)

            def load(i, b, part, first, last, landed):
                sp.dma_start(part[b][:, :], tab[bass.ds(i * P, P), first:last]).then_inc(landed[b], 16)

            def load_a(i, b):
                if not known(i, 2):
                    wait_alone(sp, passed,
                               (k_in[b], CK * uses(i - 2, b)),
                               (adj_in[b], CK * uses(i - 2, b)),
                               (q_in[b], uses(i - 2, b)),
                               (maskT_done, i - 1))
                load(i, b, tab_a, TAB_K, TAB_V, tab_a_in)

            def load_b(i, b):
                if not known(i, 2):
                    wait_alone(sp, passed,
                               (v_in[b], CK * uses(i - 2, b)),
                               (stat_done, 2 * i - 2))
                load(i, b, tab_b, TAB_V, TAB_OUT, tab_b_in)

            def load_c(i, b):
                if not known(i, 2):
                    wait_alone(sp, passed, (ctx_stored, (i - 1) * 16))
                load(i, b, tab_c, TAB_OUT, TAB, tab_c_in)

            def step(i, b):
                load_a(i + 3, 1 - b)
                load_b(i + 2, b)
                load_c(i + 1, 1 - b)

            for b in range(2):
                load_a(b, b)
                load_b(b, b)
            load_a(2, 0)
            load_c(0, 0)
            for b in range(2):
                step(b, b)
            with sp.Fori(1, items // 2) as pair:
                for b in range(2):
                    step(pair * 2 + b, b)
            for b in range(2):
                sp.wait_ge(tab_a_in[b], (items // 2 + 2 - b) * 16)
                sp.wait_ge(tab_b_in[b], (items // 2 + 1) * 16)
                sp.wait_ge(tab_c_in[b], (items // 2 + 1 - b) * 16)

        @block.gpsimd
        def _(pool):
            pool.wait_ge(const_in, 32)

            def gather(out, src, index):
                return pool.indirect_dma_start(out=out, out_offset=None, in_=src,
                                               in_offset=bass.IndirectOffsetOnAxis(ap=index.bitcast(U32), axis=0))

            def load_kq(i, b):
                used = [] if known(i, 2) else [
                    (tr_done, (i - 1) * 5),
                    (maskT_done, i - 1),
                    (s_done, (i - 1) * H)]
                wait_alone(pool, passed, (tab_a_in[b], uses(i, b)), *used)
                for c in range(CK):
                    gather(adj[b][:, c, :], adj_tab, tab_a[b][:, TAB_ADJ + c:TAB_ADJ + c + 1]).then_inc(adj_in[b], 16)
                for c in range(CK):
                    gather(k[b][:, c, :], k_tab, tab_a[b][:, TAB_K + c:TAB_K + c + 1]).then_inc(k_in[b], 16)
                gather(qT[b][:, :, :].rearrange("p c q -> p (c q)"), q_tab, tab_a[b][:, TAB_Q:TAB_Q + 1])\
                    .then_inc(q_in[b], 16)

            def load_v(i, b):
                used = [] if known(i, 2) else [(pv_done, (i - 1) * H)]
                wait_alone(pool, passed, (tab_b_in[b], uses(i, b)), *used)
                for c in range(CK):
                    gather(v[b][:, c, :], v_tab, tab_b[b][:, c:c + 1]).then_inc(v_in[b], 16)

            def store(i, b):
                wait_alone(pool, passed, (tab_c_in[b], uses(i, b)),
                           (ctx_stored, i * 16),
                           (c_done, i + 1))
                pool.indirect_dma_start(out=ctx_out, out_offset=bass.IndirectOffsetOnAxis(ap=tab_c[b][:, 0:1].bitcast(U32), axis=0),
                                        in_=cout[b][:, :], in_offset=None).then_inc(ctx_stored, 16)

            def step(i, b):
                load_kq(i + 2, b)
                load_v(i + 1, 1 - b)
                if not known(i, 1):
                    store(i - 1, 1 - b)

            for b in range(2):
                load_kq(b, b)
            load_v(0, 0)
            for b in range(2):
                step(b, b)
            with pool.Fori(1, items // 2) as pair:
                for b in range(2):
                    step(pair * 2 + b, b)
            store(items - 1, 1)
            pool.wait_ge(ctx_stored, items * 16)
            for b in range(2):
                pool.wait_ge(adj_in[b], (items // 2 + 1) * CK * 16)
                pool.wait_ge(k_in[b], (items // 2 + 1) * CK * 16)
                pool.wait_ge(q_in[b], (items // 2 + 1) * 16)
            pool.wait_ge(v_in[0], (items // 2 + 1) * CK * 16)

        @block.tensor
        def _(pe):
            pe.wait_ge(const_in, 32)

            def tr(a, b, n):
                at = a * 5 + n
                if n == 0:
                    pe.wait_ge(maskT_done, a + 1)
                if n == 1:
                    pe.wait_ge(k_in[b], CK * uses(a, b))
                if not (isinstance(at, int) and at < 2):
                    pe.wait_ge(tr_read, at - 1)
                bank = (b + n) % 2
                for c in range(CK):
                    src = maskT[b][:, c, :] if n == 0 else k[b][:, c, (n - 1) * P:n * P]
                    mm = pe.transpose(tr_ps[:, bank, c * P:(c + 1) * P], src, ident[:, :])
                mm.then_inc(tr_done, 1)

            def scores(a, b, h):
                if h == 0:
                    pe.wait_ge(q_in[b], uses(a, b))
                if h % 2 == 0:
                    pe.wait_ge(tr_read, a * 5 + h // 2 + 2)
                at = a * H + h
                if not (isinstance(at, int) and at < 2):
                    pe.wait_ge(s_read, at - 1)
                r = (h % 2) * DK
                pe.matmul(s_ps[:, h % 2, :], qT[b][r:r + DK, h // 2, :], kT[b][r:r + DK, h // 2, :],
                          start=True, stop=True).then_inc(s_done, 1)

            def probT(i, b, h):
                at = i * H + h
                pe.wait_ge(p_done, at + 1)
                if not (isinstance(at, int) and at < 2):
                    pe.wait_ge(pT_read, at - 1)
                for c in range(CK):
                    mm = pe.transpose(pT_ps[:, h % 2, c * P:(c + 1) * P], s[b][:, h, c * P:(c + 1) * P], ident[:, :])
                mm.then_inc(pT_done, 1)

            def values(i, b, h, slot):
                pe.wait_ge(pT_read, i * H + h + 1)
                if h == 0:
                    pe.wait_ge(v_in[b], CK * uses(i, b))
                if h == 0 and not known(i, 2):
                    pe.wait_ge(o_done, i - 1)
                for c in range(CK):
                    mm = pe.matmul(o_ps[:, b, h * DK:(h + 1) * DK], pT[:, slot, c, :],
                                   v[b][:, c, h * DK:(h + 1) * DK], start=c == 0, stop=c == CK - 1)
                mm.then_inc(pv_done, 1)

            def step(i, b):
                for n in range(H + 2):
                    if n < 5:
                        tr(i + 1, 1 - b, n)
                    if n < H:
                        probT(i, b, n)
                    if 1 <= n <= H:
                        values(i, b, n - 1, (n - 1) % 2)
                    if n >= 2:
                        scores(i + 1, 1 - b, n - 2)

            for n in range(5):
                tr(0, 0, n)
            for h in range(H):
                scores(0, 0, h)
            for b in range(2):
                step(b, b)
            with pe.Fori(1, items // 2) as pair:
                i2 = pair * 2
                for b in range(2):
                    step(i2 + b, b)

        @block.scalar
        def _(act):
            def tr(a, b, n):
                act.wait_ge(tr_done, a * 5 + n + 1)
                if n == 0 and not known(a, 2):
                    act.wait_ge(s_read, (a - 1) * H)
                if n == 1 and not known(a, 2):
                    act.wait_ge(s_done, (a - 1) * H)
                out = mask[b][:, :] if n == 0 else kT[b][:, n - 1, :]
                act.activation(out, tr_ps[:, (b + n) % 2, :], ACT.Copy).then_inc(tr_read, 1)

            def alphas(a, b, half):
                hs = slice(4 * half, 4 * half + 4)
                act.wait_ge(stat_done, 2 * a + half + 1)
                if half == 0 and not known(a, 2):
                    act.wait_ge(o_done, a - 1)
                act.activation(alpha[b][:, hs], mdiff[b][:, hs], ACT.Exp, scale=SCALE).then_inc(alpha_done, 1)

            def probs(a, b, h):
                if h % 4 == 0:
                    alphas(a, b, h // 4)
                act.activation(s[b][:, h, :], s[b][:, h, :], ACT.Exp, bias=negm[b][:, h:h + 1], scale=SCALE,
                               accum_out=gsum[b][:, h:h + 1]).then_inc(p_done, 1)

            def probT(i, b, h, slot):
                at = i * H + h
                act.wait_ge(pT_done, at + 1)
                if not (isinstance(at, int) and at < 2):
                    act.wait_ge(pv_done, at - 1)
                act.activation(pT[:, slot, :, :].rearrange("p c q -> p (c q)"), pT_ps[:, h % 2, :], ACT.Copy)\
                   .then_inc(pT_read, 1)

            def step(i, b):
                for n in range(H + 2):
                    if n < 4:
                        probs(i, b, 4 + n)
                    if n < 5:
                        tr(i + 1, 1 - b, n)
                    if n < H:
                        probT(i, b, n, n % 2)
                    if n >= 6:
                        probs(i + 1, 1 - b, n - 6)

            for n in range(5):
                tr(0, 0, n)
            for h in range(4):
                probs(0, 0, h)
            for b in range(2):
                step(b, b)
            with act.Fori(1, items // 2) as pair:
                i2 = pair * 2
                for b in range(2):
                    step(i2 + b, b)

        @block.vector
        def _(dve):
            dve.memset(mrun[:, :], 0.0).then_inc(init, 1)
            dve.memset(lrun[:, :], 0.0).then_inc(init, 1)
            dve.memset(orun[:, :, :], 0.0).then_inc(init, 1)
            dve.wait_ge(init, 3)
            dve.wait_ge(const_in, 32)
            STAT, MASKS, MERGE = 4, 5, 6
            LINKS = 2 * STAT + MASKS + MERGE

            def link(ins, at):
                ins.then_inc(chain, 1)
                dve.wait_ge(chain, at)

            def masks(a, b, at):
                dve.wait_ge(tab_a_in[b], uses(a, b))
                dve.wait_ge(adj_in[b], CK * uses(a, b))
                if not known(a, 2):
                    dve.wait_ge(tr_done, (a - 2) * 5 + 1)
                for c in range(CK):
                    dve.scalar_tensor_tensor(maskT[b][:, c, :], iota[:, :], tab_a[b][:, TAB_REL + c:TAB_REL + c + 1].bitcast(F32),
                                             adj[b][:, c, :], op0=ALU.is_equal, op1=ALU.add).then_inc(chain, 1)
                dve.wait_ge(chain, at + CK)
                dve.tensor_scalar(maskT[b][:, :, :], maskT[b][:, :, :], 0.0, MASKED, op0=ALU.is_equal, op1=ALU.mult)\
                   .then_inc(maskT_done, 1)
                dve.wait_ge(maskT_done, a + 1)

            def scores(a, b, h):
                if h == 0:
                    dve.wait_ge(tr_read, a * 5 + 1)
                    if not known(a, 2):
                        dve.wait_ge(pT_done, (a - 1) * H)
                wait_alone(dve, passed, (s_done, a * H + h + 1))
                dve.tensor_tensor_reduce(out=s[b][:, h, :], in0=s_ps[:, h % 2, :], in1=mask[b][:, :], scale=1.0,
                                         scalar=-3e38, op0=ALU.add, op1=ALU.max,
                                         accum_out=gmax[b][:, h:h + 1]).then_inc(s_read, 1)

            def stats(a, b, half, at):
                hs = slice(4 * half, 4 * half + 4)
                dve.wait_ge(s_read, a * H + 4 * half + 4)
                if half == 0:
                    dve.wait_ge(tab_b_in[b], uses(a, b))
                if half == 0 and not known(a, 2):
                    dve.wait_ge(p_done, (a - 1) * H)
                link(dve.tensor_scalar(mold[:, hs], mrun[:, hs], tab_b[b][:, TAB_KEEP - TAB_V:TAB_KEEP - TAB_V + 1].bitcast(F32),
                                       tab_b[b][:, TAB_RST - TAB_V:TAB_RST - TAB_V + 1].bitcast(F32), op0=ALU.mult, op1=ALU.add), at + 1)
                link(dve.tensor_tensor(mrun[:, hs], mold[:, hs], gmax[b][:, hs], ALU.max), at + 2)
                link(dve.tensor_tensor(mdiff[b][:, hs], mold[:, hs], mrun[:, hs], ALU.subtract), at + 3)
                link(dve.tensor_scalar(negm[b][:, hs], mrun[:, hs], -SCALE, None, op0=ALU.mult), at + 4)
                dve.sem_inc(stat_done, 1)

            def merge(i, b, at):
                dve.wait_ge(p_done, i * H + H)
                dve.wait_ge(alpha_done, 2 * i + 2)
                link(dve.tensor_tensor(lrun[:, :], lrun[:, :], alpha[b][:, :], ALU.mult), at + 1)
                link(dve.tensor_tensor(lrun[:, :], lrun[:, :], gsum[b][:, :], ALU.add), at + 2)
                link(dve.reciprocal(rinv[:, :], lrun[:, :]), at + 3)
                link(dve.tensor_tensor(orun[:, :, :], orun[:, :, :], alpha[b][:, :].unsqueeze(2).broadcast_to([P, H, DK]),
                                       ALU.mult), at + 4)
                dve.wait_ge(pv_done, i * H + H)
                dve.tensor_tensor(orun[:, :, :], orun[:, :, :], o_ps[:, b, :].rearrange("p (h d) -> p h d", d=DK),
                                  ALU.add).then_inc(o_done, 1)
                dve.wait_ge(o_done, i + 1)
                if not known(i, 2):
                    dve.wait_ge(ctx_stored, (i - 1) * 16)
                dve.tensor_tensor(cout[b][:, :].rearrange("p (h d) -> p h d", d=DK), orun[:, :, :],
                                  rinv[:, :].unsqueeze(2).broadcast_to([P, H, DK]), ALU.mult).then_inc(c_done, 1)
                dve.wait_ge(c_done, i + 1)

            PER = 2 * STAT + CK + 4
            FIRST = 2 * CK + 2 * STAT

            def step(i, b):
                at = i * PER + FIRST
                for n in range(2, H + 2):
                    scores(i + 1, 1 - b, n - 2)
                    if n == 5:
                        stats(i + 1, 1 - b, 0, at)
                stats(i + 1, 1 - b, 1, at + STAT)
                merge(i, b, at + 2 * STAT)
                masks(i + 2, b, at + 2 * STAT + 4)

            masks(0, 0, 0)
            masks(1, 1, CK)
            for h in range(H):
                scores(0, 0, h)
            stats(0, 0, 0, 2 * CK)
            stats(0, 0, 1, 2 * CK + STAT)
            for b in range(2):
                step(b, b)
            with dve.Fori(1, items // 2) as pair:
                i2 = pair * 2
                for b in range(2):
                    step(i2 + b, b)


def feed_forward(nc, x_rows, ctx_rows, woT, w1T, w2T, b_o, b_1, b_2, g_1, be_1, g_2, be_2, ident_in, out):
    with ExitStack() as ctx:
        sb = lambda name, shape, dt=F32: ctx.enter_context(nc.sbuf_tensor(f"ff_{name}", shape, dt))
        sem = lambda name: ctx.enter_context(nc.semaphore(f"ff_{name}"))
        ident = sb("ident", [P, P])
        wo = sb("wo", [P, CD, D])
        w1 = sb("w1", [P, CD, F])
        w2 = sb("w2", [P, CF, D])
        b1 = sb("b1", [P, CF])
        BO, G1, BE1, B2, G2, BE2 = range(6)
        vec = sb("vec", [P, 6, D])
        cx = [sb(f"cx_{b}", [P, TG, D]) for b in range(2)]
        xr = sb("xr", [P, TG, D])
        cxT = sb("cxT", [P, CD, G])
        h1 = [sb(f"h1_{b}", [P, TG, D]) for b in range(2)]
        h1T = sb("h1T", [P, CD, G])
        hid = sb("hid", [P, CF, G])
        ob = sb("ob", [P, TG, D])
        bn = sb("bn", [P, TG, 6])
        mv = sb("mv", [P, TG, 2])
        rs = sb("rs", [P, TG, 1])
        bn2 = sb("bn2", [P, TG, 6])
        mv2 = sb("mv2", [P, TG, 2])
        rs2 = sb("rs2", [P, TG, 1])
        eps = sb("eps", [P, 1])
        tr_ps = ctx.enter_context(nc.psum_tensor("ff_tr_ps", [P, 2, G], F32))
        row_ps = ctx.enter_context(nc.psum_tensor("ff_row_ps", [P, 4, D], F32))
        hid_ps = ctx.enter_context(nc.psum_tensor("ff_hid_ps", [P, 2, G], F32))
        w_in = sem("w_in")
        cx_in = [sem(f"cx_in_{b}") for b in range(2)]
        x_in = sem("x_in")
        tr_done, tr_read = sem("tr_done"), sem("tr_read")
        row_done, row_read = sem("row_done"), sem("row_read")
        hid_done, hid_read = sem("hid_done"), sem("hid_read")
        h1_done, ob_done = sem("h1_done"), sem("ob_done")
        var_done, root_done = sem("var_done"), sem("root_done")
        chain = sem("chain")
        eps_set = sem("eps_set")
        stored = sem("stored")
        passed = sem("passed")
        block = ctx.enter_context(nc.Block())
        first = lambda g: isinstance(g, int) and g == 0

        @block.sync
        def _(sp):
            sp.dma_start(ident[:, :], ident_in).then_inc(w_in, 16)
            sp.dma_start(wo[:, :, :], woT.rearrange("(c p) o -> p c o", p=P)).then_inc(w_in, 16)
            for n, v in enumerate((b_o, g_1, be_1, b_2, g_2, be_2)):
                sp.dma_start(vec[:, n, :], v.rearrange("(a o) -> a o", a=1).broadcast_to([P, D])).then_inc(w_in, 16)
            sp.dma_start(b1[:, :], b_1).then_inc(w_in, 16)

            rows = lambda ap, g: ap[bass.ds(g * G, G), :].rearrange("(t p) f -> p t f", p=P)

            def load(g, b):
                if not (isinstance(g, int) and g < 2):
                    wait_alone(sp, passed, (tr_done, (g - 2) * 2 * CD + CD))
                sp.dma_start(cx[b][:, :, :], rows(ctx_rows, g)).then_inc(cx_in[b], 16)

            def load_x(g):
                if not first(g):
                    wait_alone(sp, passed, (h1_done, g * TG))
                sp.dma_start(xr[:, :, :], rows(x_rows, g)).then_inc(x_in, 16)

            def store(g):
                wait_alone(sp, passed, (ob_done, (g + 1) * TG))
                sp.dma_start(rows(out, g), ob[:, :, :]).then_inc(stored, 16)

            load(0, 0)
            load_x(0)
            sp.dma_start(w1[:, :, :], w1T.rearrange("(c p) o -> p c o", p=P)).then_inc(w_in, 16)
            sp.dma_start(w2[:, :, :], w2T.rearrange("(c p) o -> p c o", p=P)).then_inc(w_in, 16)
            load(1, 1)
            with sp.Fori(0, NG // 2 - 1) as pair:
                g2 = pair * 2
                for b in range(2):
                    load_x(g2 + b + 1)
                    load(g2 + b + 2, b)
                    store(g2 + b)
            load_x(NG - 1)
            store(NG - 2)
            store(NG - 1)
            sp.wait_ge(stored, 16 * NG)

        ROWS = 2 * TG

        def row_at(g, kind, t):
            if kind == 0:
                return t if first(g) else TG + (g - 1) * ROWS + t
            last = isinstance(g, int) and g == NG - 1
            return TG + g * ROWS + (0 if last else TG) + t

        @block.tensor
        def _(pe):
            pe.wait_ge(w_in, 16 * 11)

            def tr(at, src, c):
                if not (isinstance(at, int) and at < 2):
                    pe.wait_ge(tr_read, at - 1)
                for t in range(TG):
                    mm = pe.transpose(tr_ps[:, c % 2, t * P:(t + 1) * P], src[:, t, c * P:(c + 1) * P], ident[:, :])
                mm.then_inc(tr_done, 1)

            def attn_rows(g, b):
                pe.wait_ge(cx_in[b], 16 * (g // 2 + 1) if isinstance(g, int) else (g - b) * 8 + 16)
                for c in range(CD):
                    tr(g * 2 * CD + c, cx[b], c)
                pe.wait_ge(tr_read, g * 2 * CD + CD)
                for t in range(TG):
                    if not (first(g) and t < 2):
                        pe.wait_ge(row_read, row_at(g, 0, t) - 1)
                    for i in range(CD):
                        mm = pe.matmul(row_ps[:, t % 2, :], cxT[:, i, t * P:(t + 1) * P], wo[:, i, :],
                                       start=i == 0, stop=i == CD - 1)
                    mm.then_inc(row_done, 1)

            def hidden(g, b):
                for t in range(TG):
                    pe.wait_ge(h1_done, g * TG + t + 1)
                for c in range(CD):
                    tr(g * 2 * CD + CD + c, h1[b], c)
                pe.wait_ge(tr_read, (g + 1) * 2 * CD)
                for f in range(CF):
                    pe.wait_ge(hid_read, g * CF + f + 1)
                    for i in range(CD):
                        mm = pe.matmul(hid_ps[:, f % 2, :], w1[:, i, f * P:(f + 1) * P], h1T[:, i, :],
                                       start=i == 0, stop=i == CD - 1)
                    mm.then_inc(hid_done, 1)

            def out_rows(g):
                pe.wait_ge(hid_read, (g + 1) * CF + 2)
                for t in range(TG):
                    pe.wait_ge(row_read, row_at(g, 1, t) - 1)
                    for i in range(CF):
                        mm = pe.matmul(row_ps[:, 2 + t % 2, :], hid[:, i, t * P:(t + 1) * P], w2[:, i, :],
                                       start=i == 0, stop=i == CF - 1)
                    mm.then_inc(row_done, 1)

            attn_rows(0, 0)
            with pe.Fori(0, NG // 2 - 1) as pair:
                g2 = pair * 2
                for b in range(2):
                    hidden(g2 + b, b)
                    attn_rows(g2 + b + 1, 1 - b)
                    out_rows(g2 + b)
            hidden(NG - 2, 0)
            attn_rows(NG - 1, 1)
            out_rows(NG - 2)
            hidden(NG - 1, 1)
            out_rows(NG - 1)

        @block.scalar
        def _(act):
            act.wait_ge(w_in, 16 * 11)
            act.wait_ge(eps_set, 1)
            act.sem_inc(hid_read, 2)

            def tr(g, kind, out):
                for c in range(CD):
                    act.wait_ge(tr_done, g * 2 * CD + kind * CD + c + 1)
                    act.activation(out[:, c, :], tr_ps[:, c % 2, :], ACT.Copy).then_inc(tr_read, 1)

            def root(g, kind, t):
                mean_var, rstd = ((mv, rs), (mv2, rs2))[kind]
                act.wait_ge(var_done, row_at(g, kind, t) + 1)
                act.activation(rstd[:, t, :], mean_var[:, t, 1:2], ACT.Sqrt, bias=eps[:, :]).then_inc(root_done, 1)

            def attn_rows(g):
                if isinstance(g, int) and g == 1:
                    act.wait_ge(row_done, TG)
                elif not first(g):
                    act.wait_ge(row_done, TG + (g - 2) * ROWS + TG)
                tr(g, 0, cxT)
                for t in range(TG):
                    root(g, 0, t)

            def out_rows(g):
                for t in range(TG - 1):
                    root(g, 1, t)

            def hidden(g):
                if not first(g):
                    act.wait_ge(hid_done, g * CF)
                tr(g, 1, h1T)
                if not first(g):
                    root(g - 1, 1, TG - 1)
                    act.wait_ge(row_done, TG + g * ROWS)
                for f in range(CF):
                    act.wait_ge(hid_done, g * CF + f + 1)
                    act.activation(hid[:, f, :], hid_ps[:, f % 2, :], ACT.Relu, bias=b1[:, f:f + 1]).then_inc(hid_read, 1)

            attn_rows(0)
            hidden(0)
            attn_rows(1)
            out_rows(0)
            with act.Fori(1, NG - 1) as g:
                hidden(g)
                attn_rows(g + 1)
                out_rows(g)
            hidden(NG - 1)
            out_rows(NG - 1)
            root(NG - 1, 1, TG - 1)

        @block.vector
        def _(dve):
            dve.wait_ge(w_in, 16 * 11)

            dve.memset(eps[:, :], EPS).then_inc(eps_set, 1)

            def norm(at, rows, out, stat, mean_var, rstd, gain, shift, sem_done, root_at):
                def link(ins):
                    nonlocal at
                    at = at + 1
                    ins.then_inc(chain, 1)
                    dve.wait_ge(chain, at)
                at = at + 1
                dve.bn_stats(stat, rows).then_inc(chain, 1)
                wait_alone(dve, passed, (chain, at))
                dve.bn_aggr(mean_var, stat).then_inc(var_done, 1)
                dve.wait_ge(root_done, root_at)
                link(dve.reciprocal(rstd, rstd))
                link(dve.tensor_scalar(rows, rows, mean_var[:, 0:1], rstd, op0=ALU.subtract, op1=ALU.mult))
                link(dve.tensor_tensor(rows, rows, vec[:, gain, :], ALU.mult))
                dve.tensor_tensor(out, rows, vec[:, shift, :], ALU.add).then_inc(sem_done, 1)

            CH1 = 6

            def chain_at(g, kind, t):
                base = row_at(g, kind, t)
                return base * CH1

            def attn_rows(g, b):
                dve.wait_ge(x_in, (g + 1) * 16)
                for t in range(TG):
                    at = chain_at(g, 0, t)
                    dve.tensor_tensor(xr[:, t, :], xr[:, t, :], vec[:, BO, :], ALU.add).then_inc(chain, 1)
                    dve.wait_ge(chain, at + 1)
                    dve.wait_ge(row_done, row_at(g, 0, t) + 1)
                    dve.tensor_tensor(xr[:, t, :], xr[:, t, :], row_ps[:, t % 2, :], ALU.add).then_inc(row_read, 1)
                    dve.wait_ge(row_read, row_at(g, 0, t) + 1)
                    if t == 0 and not (isinstance(g, int) and g < 2):
                        dve.wait_ge(tr_done, (g - 1) * 2 * CD)
                    norm(at + 1, xr[:, t, :], h1[b][:, t, :], bn[:, t, :], mv[:, t, :], rs[:, t, :], G1, BE1, h1_done, row_at(g, 0, t) + 1)
                    dve.wait_ge(h1_done, g * TG + t + 1)
                    dve.sem_inc(chain, 1)

            def out_rows(g, b):
                for t in range(TG):
                    at = chain_at(g, 1, t)
                    dve.tensor_tensor(h1[b][:, t, :], h1[b][:, t, :], vec[:, B2, :], ALU.add).then_inc(chain, 1)
                    dve.wait_ge(chain, at + 1)
                    dve.wait_ge(row_done, row_at(g, 1, t) + 1)
                    dve.tensor_tensor(h1[b][:, t, :], h1[b][:, t, :], row_ps[:, 2 + t % 2, :], ALU.add).then_inc(row_read, 1)
                    dve.wait_ge(row_read, row_at(g, 1, t) + 1)
                    if t == 0 and not first(g):
                        dve.wait_ge(stored, g * 16)
                    norm(at + 1, h1[b][:, t, :], ob[:, t, :], bn2[:, t, :], mv2[:, t, :], rs2[:, t, :], G2, BE2, ob_done, row_at(g, 1, t) + 1)
                    dve.sem_inc(chain, 1)

            attn_rows(0, 0)
            with dve.Fori(0, NG // 2 - 1) as pair:
                g2 = pair * 2
                for b in range(2):
                    attn_rows(g2 + b + 1, 1 - b)
                    out_rows(g2 + b, b)
            attn_rows(NG - 1, 1)
            out_rows(NG - 2, 0)
            out_rows(NG - 1, 1)


def layer(nc, a):
    q_tab = nc.dram_tensor("q_tab", [N, D], F32, kind="Internal").ap()
    k_tab = nc.dram_tensor("k_tab", [N, D], F32, kind="Internal").ap()
    v_tab = nc.dram_tensor("v_tab", [N, D], F32, kind="Internal").ap()
    ctx_rows = nc.dram_tensor("ctx_rows", [N, D], F32, kind="Internal").ap()
    project_qkv(nc, a["xT"], [a["wqT"], a["wkT"], a["wvT"]], a["bq"], a["bk"], a["bv"], q_tab, [k_tab, v_tab])
    attend(nc, a["tab"], a["adj_tab"], q_tab, k_tab, v_tab, ctx_rows, a["ident"], a["iota"], ITEMS)
    feed_forward(nc, a["x"], ctx_rows, a["woT"], a["w1T"], a["w2T"], a["bo"], a["b1"], a["b2"], a["g1"], a["be1"],
                 a["g2"], a["be2"], a["ident"], a["out"])


def item_table():
    tab = np.zeros((ITEMS + AHEAD, P, TAB), np.int32)
    real = tab.view(np.float32)
    p = np.arange(P)
    for i in range(ITEMS + AHEAD):
        t, g = (i // (N // KEYS), i % (N // KEYS)) if i < ITEMS else (0, 0)
        for c in range(CK):
            col = g * KEYS + c * P + p
            tab[i, :, TAB_K + c] = tab[i, :, TAB_V + c] = col
            tab[i, :, TAB_ADJ + c] = t * N + col
            real[i, :, TAB_REL + c] = col - t * P
        tab[i, :, TAB_Q] = tab[i, :, TAB_OUT] = t * P + p
        real[i, :, TAB_KEEP] = float(g > 0)
        real[i, :, TAB_RST] = 0.0 if g else -RESET
    return tab.reshape(-1, TAB)


def kernel(**inputs):
    import concourse.bacc as bacc
    from concourse.bass_utils import run_bass_kernel_spmd
    from concourse import mybir as _mybir

    given = {k.removeprefix("L0_gnn_"): np.asarray(v) for k, v in inputs.items()}
    names = {"bq": "bq", "bk": "bk", "bv": "bv", "bo": "bo", "b1": "b1", "b2": "b2",
             "g1": "ln1_g", "be1": "ln1_b", "g2": "ln2_g", "be2": "ln2_b"}
    arrays = {k: np.ascontiguousarray(given[v]) for k, v in names.items()}
    for k, v in {"wqT": "Wq", "wkT": "Wk", "wvT": "Wv", "woT": "Wo", "w1T": "W1", "w2T": "W2", "xT": "x"}.items():
        arrays[k] = np.ascontiguousarray(given[v].T)
    for k in ("bq", "b1"):
        arrays[k] = np.ascontiguousarray(arrays[k].reshape(-1, P).T)
    arrays["x"] = np.ascontiguousarray(given["x"])
    arrays["adj_tab"] = np.ascontiguousarray(given["adj"].reshape(T, P, N).transpose(0, 2, 1)).reshape(T * N, P)
    arrays["ident"] = np.eye(P, dtype=np.float32)
    arrays["iota"] = np.tile(np.arange(P, dtype=np.float32), (P, 1))
    arrays["tab"] = item_table()

    nc = bacc.Bacc("TRN2", target_bir_lowering=False, num_devices=1)
    args = {k: nc.dram_tensor(f"in_{k}", v.shape, _mybir.dt.from_np(v.dtype), kind="ExternalInput").ap()
            for k, v in arrays.items()}
    args["out"] = nc.dram_tensor("out_rows", [N, D], F32, kind="ExternalOutput").ap()
    layer(nc, args)
    r = run_bass_kernel_spmd(nc, [{f"in_{k}": v for k, v in arrays.items()}], core_ids=[0])
    return r.results[0]["out_rows"]
```

```python
import numpy as np
import concourse.bass as bass
from concourse import mybir
from contextlib import ExitStack

F32 = mybir.dt.float32
BF16 = mybir.dt.bfloat16
F16 = mybir.dt.float16
I32 = mybir.dt.int32
U32 = mybir.dt.uint32
ALU = mybir.AluOpType
ACT = mybir.ActivationFunctionType
AX = mybir.AxisListType

P = 128
N = 4096
D = 512
H = 8
DK = D // H
F = 2048
EPS = 1e-5
SCALE = DK ** -0.5
CD = D // P
CF = F // P
T = N // P
G = 512
NG = N // G
TG = G // P
CK = 4
KEYS = CK * P
MASKED = -8e9
RESET = 1e30
NB = 3
ROUNDS = (T * (N // KEYS) + NB - 1) // NB
IMAX = (ROUNDS + 2) * NB
B = N // P
LO = 64
HI = N // LO
REC_K, REC_ADJ, REC_REL, REC = 0, CK, 2 * CK, 3 * CK
REC_TILE = N // CK


def wait_alone(engine, passed, *waits):
    for semaphore, value in waits:
        engine.wait_ge(semaphore, value)
        engine.sem_inc(passed, 1)


def project_and_list(nc, a, q_tab, kv_tab, rec_tab, it_index, it_merge, rounds):
    with ExitStack() as ctx:
        sb = lambda name, shape, dt=F32: ctx.enter_context(nc.sbuf_tensor(f"qkv_{name}", shape, dt))
        sem = lambda name: ctx.enter_context(nc.semaphore(f"qkv_{name}"))
        ps = lambda name, shape: ctx.enter_context(nc.psum_tensor(f"qkv_{name}", shape, F32))
        w = [sb(f"w_{n}", [P, CD, D]) for n in "qkv"]
        bq = sb("bq", [P, CD])
        x = [sb(f"x_{b}", [P, CD, G]) for b in range(2)]
        q = [sb(f"q_{b}", [P, TG, CD, P]) for b in range(2)]
        kv = [sb(f"kv_{b}", [P, TG, 2, D]) for b in range(2)]
        HALF = B // 2
        adj = sb("adj", [P, 4, HALF, P], I32)
        own = sb("own", [P, T])
        below = sb("below", [P, P])
        iota = sb("iota", [P, P])
        column = sb("column", [P, 1])
        iota_item = sb("iota_item", [P, IMAX])
        tile_c = sb("tile_c", [HI, 3, T])
        slot = sb("slot", [HI, LO])
        number = sb("number", [P, B], F16)
        ones = sb("ones", [P, IMAX])
        inside = sb("inside", [P, TG, B])
        found = sb("found", [P, T * B])
        red = sb("red", [P, 4, HALF])
        cnt = sb("cnt", [P, TG])
        before = sb("before", [P, TG])
        total = sb("total", [P, T])
        place = sb("place", [P, TG, B])
        place_i = sb("place_i", [P, TG, B], I32)
        part_i = sb("part_i", [P, TG, B], I32)
        hi = sb("hi", [P, T * B])
        lo = sb("lo", [P, T * B])
        oh_hi = [sb(f"oh_hi_{b}", [P, B, HI], F16) for b in range(2)]
        oh_lo = [sb(f"oh_lo_{b}", [P, B, LO], F16) for b in range(2)]
        oh_n = [sb(f"oh_n_{b}", [P, B, LO], F16) for b in range(2)]
        node = sb("node", [HI, T, LO])
        TQ = T // 4
        rec = sb("rec", [HI, TQ, LO // CK, REC], I32)
        r0, r1 = (found[0:HI, n * TQ * LO:(n + 1) * TQ * LO].rearrange("h (t l) -> h t l", l=LO) for n in range(2))
        adj_flat = adj[:, :, :, :].rearrange("p n b q -> p (n b q)")
        past = adj_flat.bitcast(BF16)[:, 0:IMAX * T].rearrange("p (i t) -> p i t", t=T)
        it_tile, it_same, it_nth, it_t0, it_t1 = (
            adj_flat.bitcast(F32)[:, IMAX * T // 2 + n * IMAX:IMAX * T // 2 + (n + 1) * IMAX] for n in range(5))
        pad = sb("pad", [P, REC], I32)
        gi = sb("gi", [P, T], I32)
        gf = sb("gf", [P, T])
        cum = sb("cum", [P, T])
        rnd = sb("rnd", [P, IMAX // NB])
        q_ps = ps("q_ps", [P, 2, G])
        kv_ps = ps("kv_ps", [P, 4, D])
        l_ps = ps("l_ps", [P, 2, 512])
        BASE = 256
        w_in, c_in = sem("w_in"), sem("c_in")
        x_in = [sem(f"x_in_{b}") for b in range(2)]
        q_out = [sem(f"q_out_{b}") for b in range(2)]
        kv_out = [sem(f"kv_out_{b}") for b in range(2)]
        q_sum, q_done = sem("q_sum"), sem("q_done")
        kv_sum, kv_done = sem("kv_sum"), sem("kv_done")
        adj_in = [sem(f"adj_in_{b}") for b in range(4)]
        red_done = sem("red_done")
        found_done = sem("found_done")
        cnt_done = sem("cnt_done")
        base_done = sem("base_done")
        hi_done, lo_done = sem("hi_done"), sem("lo_done")
        number_done = sem("number_done")
        list_sum, list_done = sem("list_sum"), sem("list_done")
        chain = sem("chain")
        placed = sem("placed")
        rec_done, rec_out = sem("rec_done"), sem("rec_out")
        passed = sem("passed")
        block = ctx.enter_context(nc.Block())

        @block.sync
        def _(sp):
            def load(t, half, n):
                src = a["adj_tab"][bass.ds(t * N, N), :].rearrange("(p b) q -> p b q", b=B)
                sp.dma_start(adj[:, n, :, :], src[:, half * HALF:(half + 1) * HALF, :]).then_inc(adj_in[n], 16)

            for n, name in enumerate(("wqT", "wkT", "wvT")):
                sp.dma_start(w[n][:, :, :], a[name].rearrange("(c p) o -> p c o", p=P)).then_inc(w_in, 16)
            sp.dma_start(bq[:, :], a["bq"]).then_inc(w_in, 16)
            for n in range(4):
                load(n // 2, n % 2, n)
            with sp.Fori(1, T // 2) as pair:
                for n in range(4):
                    wait_alone(sp, passed, (red_done, pair * 4 + n - 3))
                    load(pair * 2 + n // 2, n % 2, n)
            for n in range(4):
                sp.wait_ge(rec_done, n + 1)
                sp.dma_start(rec_tab[0:T * REC_TILE, :].rearrange("(t h r) w -> h t (r w)", h=HI, r=LO // CK)[:, n * TQ:(n + 1) * TQ, :],
                             rec[:, :, :, :].rearrange("h t r w -> h t (r w)")).then_inc(rec_out, 16)
            sp.wait_ge(rec_done, 5)
            sp.dma_start(rec_tab[T * REC_TILE:T * REC_TILE + P, :], pad[:, :]).then_inc(rec_out, 16)
            sp.wait_ge(rec_out, 16 * 5)
            for b in range(2):
                sp.wait_ge(q_out[b], 16 * NG // 2)
                sp.wait_ge(kv_out[b], 16 * NG // 2)

        @block.gpsimd
        def _(pool):
            def load(g, b):
                pool.dma_start(x[b][:, :, :], a["xT"][:, bass.ds(g * G, G)].rearrange("(c p) n -> p c n", p=P))\
                    .then_inc(x_in[b], 16)

            def store(g, b):
                wait_alone(pool, passed, (q_done, (g + 1) * CD))
                pool.dma_start(q_tab[bass.ds(g * G, G), :].rearrange("(t p) f -> p t f", p=P),
                               q[b][:, :, :, :].rearrange("p t c q -> p t (c q)")).then_inc(q_out[b], 16)
                wait_alone(pool, passed, (kv_done, (g + 1) * 2 * TG))
                pool.dma_start(kv_tab[bass.ds(g * G, G), :].rearrange("(t p) f -> p t f", p=P),
                               kv[b][:, :, :, :].rearrange("p t c q -> p t (c q)")).then_inc(kv_out[b], 16)

            def numbers(batch):
                for i in range(TG):
                    wait_alone(pool, passed, (lo_done, batch * TG + i + 1))
                    pool.tensor_tensor(oh_n[i % 2][:, :, :], oh_lo[i % 2][:, :, :],
                                       number[:, :].unsqueeze(2).broadcast_to([P, B, LO]), ALU.mult).then_inc(number_done, 1)

            load(0, 0)
            load(1, 1)
            for dst, name in ((own, "own"), (below, "below"), (iota, "iota"), (column, "column"),
                              (iota_item, "iota_item"), (slot, "slot"), (number, "number")):
                pool.dma_start(dst[:, :], a[name]).then_inc(c_in, 16)
            pool.dma_start(tile_c[:, :, :], a["tile_c"]).then_inc(c_in, 16)
            store(0, 0)
            load(2, 0)
            with pool.Fori(0, NG // 2 - 2) as pair:
                for b in range(2):
                    numbers(pair * 2 + b)
                    store(pair * 2 + b + 1, 1 - b)
                    load(pair * 2 + b + 3, 1 - b)
            numbers(NG - 4)
            store(NG - 3, 1)
            load(NG - 1, 1)
            numbers(NG - 3)
            store(NG - 2, 0)
            numbers(NG - 2)
            store(NG - 1, 1)
            numbers(NG - 1)

        @block.tensor
        def _(pe):
            pe.wait_ge(w_in, 16 * 4)

            def lists(batch, i):
                t, b = batch * TG + i, i % 2
                pe.wait_ge(hi_done, t + 1)
                pe.wait_ge(number_done, t + 1)
                if not (isinstance(t, int) and t < 2):
                    pe.wait_ge(list_done, t - 1)
                for n in range(B):
                    mm = pe.matmul(l_ps[0:HI, b, 0:LO], oh_hi[b][:, n, :], oh_n[b][:, n, :], start=n == 0, stop=n == B - 1)
                mm.then_inc(list_sum, 1)

            def group(g, b):
                first = isinstance(g, int) and g == 0
                pe.wait_ge(x_in[b], g * 8 + 16 - 8 * b)
                for c in range(CD):
                    if not (first and c < 2):
                        pe.wait_ge(q_done, g * CD + c - 1)
                    for i in range(CD):
                        mm = pe.matmul(q_ps[:, c % 2, :], w[0][:, i, c * P:(c + 1) * P], x[b][:, i, :],
                                       start=i == 0, stop=i == CD - 1)
                    mm.then_inc(q_sum, 1)
                for t in range(TG):
                    for n in range(2):
                        at = 2 * t + n
                        if at >= 4 or not first:
                            pe.wait_ge(kv_done, g * 2 * TG + at - 3)
                        for i in range(CD):
                            mm = pe.matmul(kv_ps[:, at % 4, :], x[b][:, i, t * P:(t + 1) * P], w[1 + n][:, i, :],
                                           start=i == 0, stop=i == CD - 1)
                        mm.then_inc(kv_sum, 1)
                    if not first:
                        lists(g - 1, t)
                pe.wait_ge(cnt_done, g + 1)
                if not first:
                    pe.wait_ge(list_done, g * TG)
                pe.matmul(l_ps[:, 0, BASE:BASE + TG], below[:, :], cnt[:, :], start=True, stop=True)
                pe.matmul(l_ps[:, 0, BASE + TG:BASE + 2 * TG], ones[:, 0:P], cnt[:, :], start=True, stop=True).then_inc(base_done, 1)

            group(0, 0)
            group(1, 1)
            with pe.Fori(1, NG // 2) as pair:
                for b in range(2):
                    group(pair * 2 + b, b)
            for t in range(TG):
                lists(NG - 1, t)

        @block.scalar
        def _(act):
            act.wait_ge(w_in, 16 * 4)

            def lists(batch, i):
                t = batch * TG + i
                act.wait_ge(list_sum, t + 1)
                act.sem_inc(passed, 1)
                act.activation(node[:, bass.ds(t, 1), :], l_ps[0:HI, i % 2, 0:LO].unsqueeze(1), ACT.Copy).then_inc(list_done, 1)

            def group(g, b):
                early = isinstance(g, int) and g < 2
                if not early:
                    act.wait_ge(q_out[b], g * 8 - 8 * b)
                for c in range(CD):
                    act.wait_ge(q_sum, g * CD + c + 1)
                    act.activation(q[b][:, :, c, :], q_ps[:, c % 2, :].rearrange("p (t q) -> p t q", q=P),
                                   ACT.Identity, bias=bq[:, c:c + 1]).then_inc(q_done, 1)
                if not early:
                    act.wait_ge(kv_out[b], g * 8 - 8 * b)
                for t in range(TG):
                    for n in range(2):
                        at = 2 * t + n
                        act.wait_ge(kv_sum, g * 2 * TG + at + 1)
                        act.activation(kv[b][:, t, n, :], kv_ps[:, at % 4, :], ACT.Copy).then_inc(kv_done, 1)
                    if not (isinstance(g, int) and g == 0):
                        lists(g - 1, t)

            group(0, 0)
            group(1, 1)
            with act.Fori(1, NG // 2) as pair:
                for b in range(2):
                    group(pair * 2 + b, b)
            for t in range(TG):
                lists(NG - 1, t)

        @block.vector
        def _(dve):
            at = 0

            def link(ins):
                nonlocal at
                at = at + 1
                ins.then_inc(chain, 1)
                dve.wait_ge(chain, at)

            dve.wait_ge(c_in, 16 * 8)
            link(dve.memset(ones[:, :], 1.0))
            link(dve.memset(inside[:, :, :], 1.0))
            link(dve.memset(inside[:, :, 0:1], 0.0))
            batch_from = at
            LINKS = 9

            def flags(t, n, seen):
                dve.wait_ge(adj_in[n], seen * 16 + 16)
                dve.tensor_reduce(red[:, n, :], adj[:, n, :, :], AX.X, ALU.max, apply_absolute_value=True).then_inc(red_done, 1)
                dve.wait_ge(red_done, t * 2 + n % 2 + 1)
                dve.tensor_scalar(found[:, bass.ds(t * B + n % 2 * HALF, HALF)], red[:, n, :], 0.0, own[:, bass.ds(t, 1)],
                                  op0=ALU.not_equal, op1=ALU.max).then_inc(found_done, 1)

            def one_hot(batch, i):
                t, b = batch * TG + i, i % 2
                if not (isinstance(t, int) and t < 2):
                    dve.wait_ge(list_sum, t - 1)
                wide = lambda ap: ap[:, bass.ds(t * B, B)].unsqueeze(2).broadcast_to([P, B, LO])
                counted = iota[:, 0:LO].unsqueeze(1).broadcast_to([P, B, LO])
                dve.tensor_tensor(oh_lo[b][:, :, :], wide(lo), counted, ALU.is_equal).then_inc(lo_done, 1)
                dve.tensor_tensor(oh_hi[b][:, :, :], wide(hi), counted, ALU.is_equal).then_inc(hi_done, 1)

            def places(n):
                nonlocal at
                at = n * LINKS + batch_from
                marks = found[:, bass.ds(n * (TG * B), TG * B)].rearrange("p (t b) -> p t b", b=B)
                flat = lambda ap: ap[:, :, :].rearrange("p t b -> p (t b)")
                dve.wait_ge(found_done, n * (2 * TG) + 2 * TG)
                dve.tensor_reduce(cnt[:, :], marks, AX.X, ALU.add).then_inc(cnt_done, 1)
                link(dve.tensor_tensor_scan(flat(place), flat(inside), found[:, bass.ds(n * (TG * B), TG * B)], 0.0,
                                            op0=ALU.mult, op1=ALU.add))
                dve.wait_ge(base_done, n + 1)
                link(dve.tensor_copy(before[:, :], l_ps[:, 0, BASE:BASE + TG]))
                link(dve.tensor_copy(total[:, bass.ds(n * TG, TG)], l_ps[:, 0, BASE + TG:BASE + 2 * TG]))
                link(dve.tensor_tensor(place[:, :, :], place[:, :, :], before[:, :].unsqueeze(2).broadcast_to([P, TG, B]), ALU.add))
                link(dve.tensor_tensor(place[:, :, :], place[:, :, :], marks, ALU.mult))
                link(dve.tensor_scalar(place_i[:, :, :], place[:, :, :], -1.0, None, op0=ALU.add))
                link(dve.tensor_scalar(part_i[:, :, :], place_i[:, :, :], LO.bit_length() - 1, None, op0=ALU.arith_shift_right))
                dve.tensor_copy(hi[:, bass.ds(n * (TG * B), TG * B)], flat(part_i)).then_inc(chain, 1)
                link(dve.tensor_scalar(place_i[:, :, :], place_i[:, :, :], LO - 1, None, op0=ALU.bitwise_and))
                dve.wait_ge(chain, at + 1)
                dve.tensor_copy(lo[:, bass.ds(n * (TG * B), TG * B)], flat(place_i)).then_inc(placed, 1)
                dve.wait_ge(placed, n + 1)

            for i in range(TG):
                for half in range(2):
                    flags(i, i % 2 * 2 + half, i // 2)
            places(0)

            def batch(n):
                for i in range(TG):
                    for half in range(2):
                        flags(n * TG + i, i % 2 * 2 + half, n * (TG // 2) + i // 2)
                    one_hot(n - 1, i)
                places(n)

            batch(1)
            with dve.Fori(2, NG) as n:
                batch(n)
            at = batch_from + NG * LINKS
            for i in range(TG):
                one_hot(NG - 1, i)

            link(dve.tensor_scalar(gi[:, :], total[:, :], float(KEYS - 1), None, op0=ALU.add))
            link(dve.tensor_scalar(gi[:, :], gi[:, :], KEYS.bit_length() - 1, None, op0=ALU.arith_shift_right))
            link(dve.tensor_copy(gf[:, :], gi[:, :]))
            link(dve.tensor_tensor_scan(cum[:, :], ones[:, 0:T], gf[:, :], 0.0, op0=ALU.mult, op1=ALU.add))
            link(dve.tensor_tensor(past, cum[:, :].unsqueeze(1).broadcast_to([P, IMAX, T]),
                                   iota_item[:, :].unsqueeze(2).broadcast_to([P, IMAX, T]), ALU.is_le))
            link(dve.tensor_reduce(it_tile, past, AX.X, ALU.add))
            link(dve.memset(it_same, 0.0))
            link(dve.tensor_tensor(it_same[:, 1:IMAX], it_tile[:, 1:IMAX], it_tile[:, 0:IMAX - 1], ALU.is_equal))
            link(dve.tensor_tensor_scan(it_nth, ones[:, 0:IMAX], it_same, 0.0, op0=ALU.add, op1=ALU.mult))
            link(dve.tensor_scalar(it_t0, it_nth, float(P), None, op0=ALU.mult))
            link(dve.scalar_tensor_tensor(it_t0, it_tile, float(REC_TILE), it_t0, op0=ALU.mult, op1=ALU.add))
            link(dve.tensor_scalar(it_index[:, 0, :], it_t0, float(T * REC_TILE), column[:, 0:1], op0=ALU.min, op1=ALU.add))
            link(dve.tensor_scalar(it_t1, it_tile, float(T - 1), float(P), op0=ALU.min, op1=ALU.mult))
            link(dve.tensor_scalar(it_index[:, 1, :], it_t1, column[:, 0:1], None, op0=ALU.add))
            link(dve.scalar_tensor_tensor(it_merge[:, 0, :], it_tile, T - 0.5, it_same, op0=ALU.is_gt, op1=ALU.max))
            link(dve.tensor_scalar(it_merge[:, 1, :], it_merge[:, 0, :], -1.0, RESET, op0=ALU.add, op1=ALU.mult))
            link(dve.tensor_scalar(rnd[:, :], iota_item[:, 0:IMAX:NB], cum[:, T - 1:T], None, op0=ALU.is_lt))
            link(dve.tensor_reduce(gf[:, 0:1], rnd[:, :], AX.X, ALU.add))
            link(dve.tensor_copy(rounds[:, 0:1], gf[:, 0:1]))
            link(dve.tensor_scalar(rounds[:, 1:2], gf[:, 0:1], -1.0, None, op0=ALU.add))
            link(dve.memset(pad[:, REC_K:REC_ADJ], 0))
            link(dve.memset(pad[:, REC_ADJ:REC_REL], T * N))
            link(dve.memset(pad[:, REC_REL:REC].bitcast(F32), -1.0))

            for n in range(4):
                last = (n + 1) * TQ
                dve.wait_ge(list_done, last)
                if n:
                    dve.wait_ge(rec_out, 16 * n)
                nd = node[:, n * TQ:last, :]
                col = lambda ap: ap.unsqueeze(2).broadcast_to([HI, TQ, LO])
                part = lambda c: rec[:, :, :, c:c + CK]
                r4 = lambda ap: ap.rearrange("h t (r c) -> h t r c", c=CK)
                link(dve.tensor_tensor(r0, slot[:, :].unsqueeze(1).broadcast_to([HI, TQ, LO]), col(total[0:HI, n * TQ:last]), ALU.is_lt))
                link(dve.scalar_tensor_tensor(nd, nd, float(N // 2 + 1), r0, op0=ALU.add, op1=ALU.mult))
                link(dve.tensor_scalar(part(REC_K), r4(nd), -1.0, 0.0, op0=ALU.add, op1=ALU.max))
                link(dve.tensor_scalar(r0, nd, 0.0, None, op0=ALU.is_equal))
                link(dve.tensor_tensor(r0, r0, col(tile_c[:, 1, n * TQ:last]), ALU.mult))
                link(dve.tensor_tensor(r1, nd, col(tile_c[:, 0, n * TQ:last]), ALU.add))
                link(dve.tensor_tensor(part(REC_ADJ), r4(r0), r4(r1), ALU.add))
                link(dve.tensor_tensor(part(REC_REL).bitcast(F32), r4(nd), r4(col(tile_c[:, 2, n * TQ:last])), ALU.add))
                dve.sem_inc(rec_done, 1)
            dve.sem_inc(rec_done, 1)


def attend(nc, adj_tab, q_tab, kv_tab, rec_tab, it_index, it_merge, rounds, b_k, ctx_out, ident_in, iota_in):
    with ExitStack() as ctx:
        sb = lambda name, shape, dt=F32: ctx.enter_context(nc.sbuf_tensor(f"att_{name}", shape, dt))
        ring = lambda name, shape, dt=F32: [sb(f"{name}_{b}", shape, dt) for b in range(NB)]
        ps = lambda name, shape: ctx.enter_context(nc.psum_tensor(f"att_{name}", shape, F32))
        sem = lambda name: ctx.enter_context(nc.semaphore(f"att_{name}"))
        sems = lambda name: [sem(f"{name}_{b}") for b in range(NB)]
        ident = sb("ident", [P, P])
        iota = sb("iota", [P, P])
        bk = sb("bk", [P, CD])
        index = ring("index", [P, 2], I32)
        index_out = ring("index_out", [P, 1], I32)
        rec = ring("rec", [P, REC], I32)
        kv = ring("kv", [P, CK, 2 * D])
        adj = ring("adj", [P, CK, P], I32)
        qT = ring("qT", [P, CD, P])
        maskT = ring("maskT", [P, CK, P])
        mask = ring("mask", [P, KEYS])
        kT = ring("kT", [P, CD, KEYS])
        s = ring("s", [P, H, KEYS])
        pT = sb("pT", [P, 2, CK, P])
        gmax = ring("gmax", [P, H])
        mold = sb("mold", [P, H])
        mrun = sb("mrun", [P, H])
        mdiff = ring("mdiff", [P, H])
        negm = ring("negm", [P, H])
        alpha = ring("alpha", [P, H])
        gsum = ring("gsum", [P, H])
        lrun = sb("lrun", [P, H])
        rinv = sb("rinv", [P, H])
        orun = sb("orun", [P, H, DK])
        cout = ring("cout", [P, D])
        tr_ps = ps("tr_ps", [P, 2, KEYS])
        s_ps = ps("s_ps", [P, 2, KEYS])
        pT_ps = ps("pT_ps", [P, 2, KEYS])
        o_ps = ps("o_ps", [P, 2, D])
        const_in = sem("const_in")
        rec_in, kv_in, adj_in, q_in = sems("rec_in"), sems("kv_in"), sems("adj_in"), sems("q_in")
        index_done = sem("index_done")
        out_index = sem("out_index")
        ctx_stored = sem("ctx_stored")
        maskT_done = sem("maskT_done")
        tr_done = sem("tr_done")
        tr_read = sem("tr_read")
        s_done = sem("s_done")
        s_read = sem("s_read")
        stat_done = sem("stat_done")
        alpha_done = sem("alpha_done")
        p_done = sem("p_done")
        pT_done = sem("pT_done")
        pT_read = sem("pT_read")
        pv_done = sem("pv_done")
        o_done = sem("o_done")
        c_done = sem("c_done")
        init = sem("init")
        chain = sem("chain")
        passed = sem("passed")
        block = ctx.enter_context(nc.Block())
        HH = H // 2
        TR = 1 + CD

        class Item:

            def __init__(self, k, b):
                self.k, self.b = k + b // NB, b % NB
                self.i = self.k * NB + self.b
                self.first = isinstance(self.k, int) and self.k == 0
                self.uses = self.k * 16 + 16

            def ahead(self, n):
                return Item(self.k, self.b + n)

        def each_step(engine, step, count):
            for b in range(NB):
                step(Item(0, b))
            with engine.Fori(1, count) as k:
                for b in range(NB):
                    step(Item(k, b))

        @block.sync
        def _(sp):
            sp.dma_start(ident[:, :], ident_in).then_inc(const_in, 16)
            sp.dma_start(iota[:, :], iota_in).then_inc(const_in, 16)
            sp.dma_start(bk[:, :], b_k).then_inc(const_in, 16)

        @block.gpsimd
        def _(pool):
            count = pool.value_load(rounds[0:1, 0:1], min_val=2, max_val=ROUNDS)
            last = pool.value_load(rounds[0:1, 1:2], min_val=1, max_val=ROUNDS - 1)

            def gather(out, src, index):
                return pool.indirect_dma_start(out=out, out_offset=None, in_=src,
                                               in_offset=bass.IndirectOffsetOnAxis(ap=index.bitcast(U32), axis=0))

            def load_rec(it):
                if not it.first:
                    wait_alone(pool, passed,
                               (maskT_done, it.i - NB + 1),
                               (kv_in[it.b], it.k * (16 * CK)),
                               (q_in[it.b], it.k * 16))
                pool.tensor_copy(index[it.b][:, :], it_index[:, :, bass.ds(it.i, 1)].rearrange("p n i -> p (n i)"))\
                    .then_inc(index_done, 1)
                wait_alone(pool, passed, (index_done, it.i + 1))
                gather(rec[it.b][:, :], rec_tab, index[it.b][:, 0:1]).then_inc(rec_in[it.b], 16)

            def load_adj(it):
                wait_alone(pool, passed, (rec_in[it.b], it.uses))
                for c in range(CK):
                    gather(adj[it.b][:, c, :], adj_tab, rec[it.b][:, REC_ADJ + c:REC_ADJ + c + 1]).then_inc(adj_in[it.b], 16)

            def load(it):
                if not it.first:
                    wait_alone(pool, passed, (s_done, (it.i - NB + 1) * H))
                gather(qT[it.b][:, :, :].rearrange("p c q -> p (c q)"), q_tab, index[it.b][:, 1:2]).then_inc(q_in[it.b], 16)
                if not it.first:
                    wait_alone(pool, passed, (pv_done, (it.i - NB + 1) * H))
                for c in range(CK):
                    gather(kv[it.b][:, c, :], kv_tab, rec[it.b][:, REC_K + c:REC_K + c + 1]).then_inc(kv_in[it.b], 16)

            def store(it):
                if not (it.first and it.b == 0):
                    wait_alone(pool, passed, (ctx_stored, it.i * 16))
                pool.tensor_copy(index_out[it.b][:, :], it_index[:, 1, bass.ds(it.i, 1)]).then_inc(out_index, 1)
                wait_alone(pool, passed, (out_index, it.i + 1), (c_done, it.i * 2 + 2))
                pool.indirect_dma_start(out=ctx_out, out_offset=bass.IndirectOffsetOnAxis(ap=index_out[it.b][:, :].bitcast(U32), axis=0),
                                        in_=cout[it.b][:, :], in_offset=None).then_inc(ctx_stored, 16)

            def step(it):
                load_rec(it.ahead(3))
                load(it.ahead(2))
                load_adj(it.ahead(3))
                if not (it.first and it.b == 0):
                    store(Item(it.k - 1 if it.b == 0 else it.k, NB - 1 if it.b == 0 else it.b - 1))

            for b in range(NB):
                load_rec(Item(0, b))
                load_adj(Item(0, b))
            load(Item(0, 0))
            load(Item(0, 1))
            each_step(pool, step, count)
            store(Item(last, NB - 1))
            wait_alone(pool, passed, (ctx_stored, count * (16 * NB)))
            for b in range(NB):
                wait_alone(pool, passed, (rec_in[b], count * 16 + 16))
                wait_alone(pool, passed, (adj_in[b], (count + 1) * (16 * CK)))
                if b < 2:
                    wait_alone(pool, passed, (kv_in[b], (count + 1) * (16 * CK)), (q_in[b], count * 16 + 16))

        @block.tensor
        def _(pe):
            pe.wait_ge(const_in, 48)
            count = pe.value_load(rounds[0:1, 0:1], min_val=2, max_val=ROUNDS)

            def unless_first(it, before, value, semaphore):
                if not (it.first and it.b == 0 and before < 2):
                    pe.wait_ge(semaphore, value)

            def tr(it, n):
                if n == 0:
                    pe.wait_ge(maskT_done, it.i + 1)
                if n == 1:
                    pe.wait_ge(kv_in[it.b], it.uses * CK)
                if n == 0 and not (it.first and it.b == 0):
                    pe.wait_ge(tr_read, it.i * TR)
                if n:
                    unless_first(it, n, it.i * TR + n - 1, tr_read)
                for c in range(CK):
                    src = maskT[it.b][:, c, :] if n == 0 else kv[it.b][:, c, (n - 1) * P:n * P]
                    mm = pe.transpose(tr_ps[:, n % 2, c * P:(c + 1) * P], src, ident[:, :])
                mm.then_inc(tr_done, 1)

            def scores(it, h):
                if h == 0:
                    pe.wait_ge(q_in[it.b], it.uses)
                if h % 2 == 0:
                    pe.wait_ge(tr_read, it.i * TR + h // 2 + 2)
                unless_first(it, h, it.i * H + h - 1, s_read)
                r = (h % 2) * DK
                pe.matmul(s_ps[:, h % 2, :], qT[it.b][r:r + DK, h // 2, :], kT[it.b][r:r + DK, h // 2, :],
                          start=True, stop=True).then_inc(s_done, 1)

            def probT(it, h):
                pe.wait_ge(p_done, it.i * H + h + 1)
                unless_first(it, h, it.i * H + h - 1, pT_read)
                for c in range(CK):
                    mm = pe.transpose(pT_ps[:, h % 2, c * P:(c + 1) * P], s[it.b][:, h, c * P:(c + 1) * P], ident[:, :])
                mm.then_inc(pT_done, 1)

            def values(it, h):
                pe.wait_ge(pT_read, it.i * H + h + 1)
                if h % HH == 0 and not (it.first and it.b == 0):
                    pe.wait_ge(o_done, it.i * 2 + h // HH - 1)
                for c in range(CK):
                    mm = pe.matmul(o_ps[:, h // HH, (h % HH) * DK:(h % HH + 1) * DK], pT[:, h % 2, c, :],
                                   kv[it.b][:, c, D + h * DK:D + (h + 1) * DK], start=c == 0, stop=c == CK - 1)
                mm.then_inc(pv_done, 1)

            def step(it):
                nxt = it.ahead(1)
                for n in range(H + 2):
                    if n < TR:
                        tr(nxt, n)
                    if n < H:
                        probT(it, n)
                    if 1 <= n <= H:
                        values(it, n - 1)
                    if n >= 2:
                        scores(nxt, n - 2)

            for n in range(TR):
                tr(Item(0, 0), n)
            for h in range(H):
                scores(Item(0, 0), h)
            each_step(pe, step, count)

        @block.scalar
        def _(act):
            act.wait_ge(const_in, 48)
            count = act.value_load(rounds[0:1, 0:1], min_val=2, max_val=ROUNDS)

            def tr(it, n):
                act.wait_ge(tr_done, it.i * TR + n + 1)
                if n == 0 and not it.first:
                    act.wait_ge(s_read, (it.i - NB + 1) * H)
                if n == 1 and not it.first:
                    act.wait_ge(s_done, (it.i - NB + 1) * H)
                src = tr_ps[:, n % 2, :]
                if n == 0:
                    act.activation(mask[it.b][:, :], src, ACT.Copy).then_inc(tr_read, 1)
                else:
                    act.activation(kT[it.b][:, n - 1, :], src, ACT.Identity, bias=bk[:, n - 1:n]).then_inc(tr_read, 1)

            def alphas(it, half):
                hs = slice(HH * half, HH * half + HH)
                act.wait_ge(stat_done, it.i * 2 + half + 1)
                if half == 0 and not it.first:
                    act.wait_ge(o_done, (it.i - NB + 1) * 2)
                act.activation(alpha[it.b][:, hs], mdiff[it.b][:, hs], ACT.Exp, scale=SCALE).then_inc(alpha_done, 1)

            def probs(it, h):
                if h % HH == 0:
                    alphas(it, h // HH)
                act.activation(s[it.b][:, h, :], s[it.b][:, h, :], ACT.Exp, bias=negm[it.b][:, h:h + 1], scale=SCALE,
                               accum_out=gsum[it.b][:, h:h + 1]).then_inc(p_done, 1)

            def probT(it, h):
                act.wait_ge(pT_done, it.i * H + h + 1)
                if not (it.first and it.b == 0 and h < 2):
                    act.wait_ge(pv_done, it.i * H + h - 1)
                act.activation(pT[:, h % 2, :, :].rearrange("p c q -> p (c q)"), pT_ps[:, h % 2, :], ACT.Copy)\
                   .then_inc(pT_read, 1)

            def step(it):
                nxt = it.ahead(1)
                for n in range(H + 2):
                    if n < TR:
                        tr(nxt, n)
                    if n < H:
                        probT(it, n)
                    if n < HH:
                        probs(it, HH + n)
                    if n >= 6:
                        probs(nxt, n - 6)

            for n in range(TR):
                tr(Item(0, 0), n)
            for h in range(HH):
                probs(Item(0, 0), h)
            each_step(act, step, count)

        @block.vector
        def _(dve):
            dve.memset(mrun[:, :], 0.0).then_inc(init, 1)
            dve.memset(lrun[:, :], 0.0).then_inc(init, 1)
            dve.memset(orun[:, :, :], 0.0).then_inc(init, 1)
            dve.wait_ge(init, 3)
            dve.wait_ge(const_in, 48)
            count = dve.value_load(rounds[0:1, 0:1], min_val=2, max_val=ROUNDS)
            STAT, MASK, MERGE = 4, CK, 4
            PER = 2 * STAT + MASK + 2 * MERGE
            AHEAD = 2 * MASK + 2 * STAT

            def link(ins, at):
                ins.then_inc(chain, 1)
                dve.wait_ge(chain, at)

            def masks(it, at):
                dve.wait_ge(rec_in[it.b], it.uses)
                dve.wait_ge(adj_in[it.b], it.uses * CK)
                if not it.first:
                    dve.wait_ge(tr_done, (it.i - NB) * TR + 1)
                for c in range(CK):
                    dve.scalar_tensor_tensor(maskT[it.b][:, c, :], iota[:, :], rec[it.b][:, REC_REL + c:REC_REL + c + 1].bitcast(F32),
                                             adj[it.b][:, c, :], op0=ALU.is_equal, op1=ALU.add).then_inc(chain, 1)
                dve.wait_ge(chain, at + CK)
                dve.tensor_scalar(maskT[it.b][:, :, :], maskT[it.b][:, :, :], 0.0, MASKED, op0=ALU.is_equal, op1=ALU.mult)\
                   .then_inc(maskT_done, 1)

            def scores(it, h):
                if h == 0:
                    dve.wait_ge(tr_read, it.i * TR + 1)
                    if not it.first:
                        dve.wait_ge(pT_done, (it.i - NB + 1) * H)
                wait_alone(dve, passed, (s_done, it.i * H + h + 1))
                dve.tensor_tensor_reduce(out=s[it.b][:, h, :], in0=s_ps[:, h % 2, :], in1=mask[it.b][:, :], scale=1.0,
                                         scalar=-3e38, op0=ALU.add, op1=ALU.max,
                                         accum_out=gmax[it.b][:, h:h + 1]).then_inc(s_read, 1)

            def stats(it, half, at):
                hs = slice(HH * half, HH * half + HH)
                dve.wait_ge(s_read, it.i * H + HH * half + HH)
                if half == 0 and not it.first:
                    dve.wait_ge(p_done, (it.i - NB + 1) * H)
                link(dve.tensor_scalar(mold[:, hs], mrun[:, hs], it_merge[:, 0, bass.ds(it.i, 1)],
                                       it_merge[:, 1, bass.ds(it.i, 1)], op0=ALU.mult, op1=ALU.add), at + 1)
                link(dve.tensor_tensor(mrun[:, hs], mold[:, hs], gmax[it.b][:, hs], ALU.max), at + 2)
                link(dve.tensor_tensor(mdiff[it.b][:, hs], mold[:, hs], mrun[:, hs], ALU.subtract), at + 3)
                link(dve.tensor_scalar(negm[it.b][:, hs], mrun[:, hs], -SCALE, None, op0=ALU.mult), at + 4)
                dve.sem_inc(stat_done, 1)

            def merge(it, half, at):
                hs = slice(HH * half, HH * half + HH)
                wide = lambda ap: ap[:, hs].unsqueeze(2).broadcast_to([P, HH, DK])
                dve.wait_ge(p_done, it.i * H + HH * half + HH)
                dve.wait_ge(alpha_done, it.i * 2 + half + 1)
                link(dve.tensor_tensor(lrun[:, hs], lrun[:, hs], alpha[it.b][:, hs], ALU.mult), at + 1)
                link(dve.tensor_tensor(lrun[:, hs], lrun[:, hs], gsum[it.b][:, hs], ALU.add), at + 2)
                link(dve.reciprocal(rinv[:, hs], lrun[:, hs]), at + 3)
                link(dve.tensor_tensor(orun[:, hs, :], orun[:, hs, :], wide(alpha[it.b]), ALU.mult), at + 4)
                dve.wait_ge(pv_done, it.i * H + HH * half + HH)
                dve.tensor_tensor(orun[:, hs, :], orun[:, hs, :],
                                  o_ps[:, half, 0:HH * DK].rearrange("p (h d) -> p h d", d=DK), ALU.add).then_inc(o_done, 1)
                dve.wait_ge(o_done, it.i * 2 + half + 1)
                if half == 0 and not it.first:
                    dve.wait_ge(ctx_stored, (it.i - NB + 1) * 16)
                dve.tensor_tensor(cout[it.b][:, :].rearrange("p (h d) -> p h d", d=DK)[:, hs, :], orun[:, hs, :],
                                  wide(rinv), ALU.mult).then_inc(c_done, 1)

            def step(it):
                nxt, at = it.ahead(1), it.i * PER + AHEAD
                for n in range(2, H + 2):
                    scores(nxt, n - 2)
                    if n == 3:
                        masks(it.ahead(2), at)
                    if n == 5:
                        stats(nxt, 0, at + MASK)
                    if n == 7:
                        merge(it, 0, at + MASK + STAT)
                stats(nxt, 1, at + MASK + STAT + MERGE)
                merge(it, 1, at + MASK + 2 * STAT + MERGE)

            masks(Item(0, 0), 0)
            masks(Item(0, 1), MASK)
            for h in range(H):
                scores(Item(0, 0), h)
            for half in range(2):
                stats(Item(0, 0), half, 2 * MASK + half * STAT)
            each_step(dve, step, count)


def feed_forward(nc, x_rows, ctx_rows, woT, w1T, w2T, b_v, b_o, b_1, b_2, g_1, be_1, g_2, be_2, ident_in, out):
    with ExitStack() as ctx:
        sb = lambda name, shape, dt=F32: ctx.enter_context(nc.sbuf_tensor(f"ff_{name}", shape, dt))
        sem = lambda name: ctx.enter_context(nc.semaphore(f"ff_{name}"))
        ident = sb("ident", [P, P])
        wo = sb("wo", [P, CD, D])
        w1 = sb("w1", [P, CD, F])
        w2 = sb("w2", [P, CF, D])
        b1 = sb("b1", [P, CF])
        bv = sb("bv", [P, CD])
        BO, G1, BE1, B2, G2, BE2 = range(6)
        vec = sb("vec", [P, 6, D])
        cx = [sb(f"cx_{b}", [P, TG, D]) for b in range(2)]
        xr = sb("xr", [P, TG, D])
        cxT = sb("cxT", [P, CD, G])
        h1 = [sb(f"h1_{b}", [P, TG, D]) for b in range(2)]
        h1T = sb("h1T", [P, CD, G])
        hid = sb("hid", [P, CF, G])
        ob = sb("ob", [P, TG, D])
        bn = sb("bn", [P, TG, 6])
        mv = sb("mv", [P, TG, 2])
        rs = sb("rs", [P, TG, 1])
        bn2 = sb("bn2", [P, TG, 6])
        mv2 = sb("mv2", [P, TG, 2])
        rs2 = sb("rs2", [P, TG, 1])
        eps = sb("eps", [P, 1])
        zero = sb("zero", [P, 1])
        tr_ps = ctx.enter_context(nc.psum_tensor("ff_tr_ps", [P, 2, G], F32))
        row_ps = ctx.enter_context(nc.psum_tensor("ff_row_ps", [P, 4, D], F32))
        hid_ps = ctx.enter_context(nc.psum_tensor("ff_hid_ps", [P, 2, G], F32))
        w_in = sem("w_in")
        cx_in = [sem(f"cx_in_{b}") for b in range(2)]
        x_in = sem("x_in")
        tr_done, tr_read = sem("tr_done"), sem("tr_read")
        row_done, row_read = sem("row_done"), sem("row_read")
        hid_done, hid_read = sem("hid_done"), sem("hid_read")
        h1_done, ob_done = sem("h1_done"), sem("ob_done")
        var_done, root_done = sem("var_done"), sem("root_done")
        chain = sem("chain")
        eps_set = sem("eps_set")
        stored = sem("stored")
        passed = sem("passed")
        block = ctx.enter_context(nc.Block())
        first = lambda g: isinstance(g, int) and g == 0

        @block.sync
        def _(sp):
            sp.dma_start(ident[:, :], ident_in).then_inc(w_in, 16)
            sp.dma_start(wo[:, :, :], woT.rearrange("(c p) o -> p c o", p=P)).then_inc(w_in, 16)
            for n, v in enumerate((b_o, g_1, be_1, b_2, g_2, be_2)):
                sp.dma_start(vec[:, n, :], v.rearrange("(a o) -> a o", a=1).broadcast_to([P, D])).then_inc(w_in, 16)
            sp.dma_start(b1[:, :], b_1).then_inc(w_in, 16)
            sp.dma_start(bv[:, :], b_v).then_inc(w_in, 16)

            rows = lambda ap, g: ap[bass.ds(g * G, G), :].rearrange("(t p) f -> p t f", p=P)

            def load(g, b):
                if not (isinstance(g, int) and g < 2):
                    wait_alone(sp, passed, (tr_done, (g - 2) * 2 * CD + CD))
                sp.dma_start(cx[b][:, :, :], rows(ctx_rows, g)).then_inc(cx_in[b], 16)

            def load_x(g):
                if not first(g):
                    wait_alone(sp, passed, (h1_done, g * TG))
                sp.dma_start(xr[:, :, :], rows(x_rows, g)).then_inc(x_in, 16)

            def store(g):
                wait_alone(sp, passed, (ob_done, (g + 1) * TG))
                sp.dma_start(rows(out, g), ob[:, :, :]).then_inc(stored, 16)

            load(0, 0)
            load_x(0)
            sp.dma_start(w1[:, :, :], w1T.rearrange("(c p) o -> p c o", p=P)).then_inc(w_in, 16)
            sp.dma_start(w2[:, :, :], w2T.rearrange("(c p) o -> p c o", p=P)).then_inc(w_in, 16)
            load(1, 1)
            with sp.Fori(0, NG // 2 - 1) as pair:
                g2 = pair * 2
                for b in range(2):
                    load_x(g2 + b + 1)
                    load(g2 + b + 2, b)
                    store(g2 + b)
            load_x(NG - 1)
            store(NG - 2)
            store(NG - 1)
            sp.wait_ge(stored, 16 * NG)

        ROWS = 2 * TG

        def row_at(g, kind, t):
            if kind == 0:
                return t if first(g) else TG + (g - 1) * ROWS + t
            last = isinstance(g, int) and g == NG - 1
            return TG + g * ROWS + (0 if last else TG) + t

        @block.tensor
        def _(pe):
            pe.wait_ge(w_in, 16 * 12)

            def tr(at, src, c):
                if not (isinstance(at, int) and at < 2):
                    pe.wait_ge(tr_read, at - 1)
                for t in range(TG):
                    mm = pe.transpose(tr_ps[:, c % 2, t * P:(t + 1) * P], src[:, t, c * P:(c + 1) * P], ident[:, :])
                mm.then_inc(tr_done, 1)

            def attn_rows(g, b):
                pe.wait_ge(cx_in[b], 16 * (g // 2 + 1) if isinstance(g, int) else (g - b) * 8 + 16)
                for c in range(CD):
                    tr(g * 2 * CD + c, cx[b], c)
                pe.wait_ge(tr_read, g * 2 * CD + CD)
                for t in range(TG):
                    if not (first(g) and t < 2):
                        pe.wait_ge(row_read, row_at(g, 0, t) - 1)
                    for i in range(CD):
                        mm = pe.matmul(row_ps[:, t % 2, :], cxT[:, i, t * P:(t + 1) * P], wo[:, i, :],
                                       start=i == 0, stop=i == CD - 1)
                    mm.then_inc(row_done, 1)

            def hidden(g, b):
                for t in range(TG):
                    pe.wait_ge(h1_done, g * TG + t + 1)
                for c in range(CD):
                    tr(g * 2 * CD + CD + c, h1[b], c)
                pe.wait_ge(tr_read, (g + 1) * 2 * CD)
                for f in range(CF):
                    pe.wait_ge(hid_read, g * CF + f + 1)
                    for i in range(CD):
                        mm = pe.matmul(hid_ps[:, f % 2, :], w1[:, i, f * P:(f + 1) * P], h1T[:, i, :],
                                       start=i == 0, stop=i == CD - 1)
                    mm.then_inc(hid_done, 1)

            def out_rows(g):
                pe.wait_ge(hid_read, (g + 1) * CF + 2)
                for t in range(TG):
                    pe.wait_ge(row_read, row_at(g, 1, t) - 1)
                    for i in range(CF):
                        mm = pe.matmul(row_ps[:, 2 + t % 2, :], hid[:, i, t * P:(t + 1) * P], w2[:, i, :],
                                       start=i == 0, stop=i == CF - 1)
                    mm.then_inc(row_done, 1)

            attn_rows(0, 0)
            with pe.Fori(0, NG // 2 - 1) as pair:
                g2 = pair * 2
                for b in range(2):
                    hidden(g2 + b, b)
                    attn_rows(g2 + b + 1, 1 - b)
                    out_rows(g2 + b)
            hidden(NG - 2, 0)
            attn_rows(NG - 1, 1)
            out_rows(NG - 2)
            hidden(NG - 1, 1)
            out_rows(NG - 1)

        @block.scalar
        def _(act):
            act.wait_ge(w_in, 16 * 12)
            act.wait_ge(eps_set, 2)
            act.sem_inc(hid_read, 2)

            def tr(g, kind, out):
                for c in range(CD):
                    act.wait_ge(tr_done, g * 2 * CD + kind * CD + c + 1)
                    bias = bv[:, c:c + 1] if kind == 0 else zero[:, :]
                    act.activation(out[:, c, :], tr_ps[:, c % 2, :], ACT.Identity, bias=bias).then_inc(tr_read, 1)

            def root(g, kind, t):
                mean_var, rstd = ((mv, rs), (mv2, rs2))[kind]
                act.wait_ge(var_done, row_at(g, kind, t) + 1)
                act.activation(rstd[:, t, :], mean_var[:, t, 1:2], ACT.Sqrt, bias=eps[:, :]).then_inc(root_done, 1)

            def attn_rows(g):
                if isinstance(g, int) and g == 1:
                    act.wait_ge(row_done, TG)
                elif not first(g):
                    act.wait_ge(row_done, TG + (g - 2) * ROWS + TG)
                tr(g, 0, cxT)
                for t in range(TG):
                    root(g, 0, t)

            def out_rows(g):
                for t in range(TG - 1):
                    root(g, 1, t)

            def hidden(g):
                if not first(g):
                    act.wait_ge(hid_done, g * CF)
                tr(g, 1, h1T)
                if not first(g):
                    root(g - 1, 1, TG - 1)
                    act.wait_ge(row_done, TG + g * ROWS)
                for f in range(CF):
                    act.wait_ge(hid_done, g * CF + f + 1)
                    act.activation(hid[:, f, :], hid_ps[:, f % 2, :], ACT.Relu, bias=b1[:, f:f + 1]).then_inc(hid_read, 1)

            attn_rows(0)
            hidden(0)
            attn_rows(1)
            out_rows(0)
            with act.Fori(1, NG - 1) as g:
                hidden(g)
                attn_rows(g + 1)
                out_rows(g)
            hidden(NG - 1)
            out_rows(NG - 1)
            root(NG - 1, 1, TG - 1)

        @block.vector
        def _(dve):
            dve.wait_ge(w_in, 16 * 12)

            dve.memset(eps[:, :], EPS).then_inc(eps_set, 1)
            dve.memset(zero[:, :], 0.0).then_inc(eps_set, 1)

            def norm(at, rows, out, stat, mean_var, rstd, gain, shift, sem_done, root_at):
                def link(ins):
                    nonlocal at
                    at = at + 1
                    ins.then_inc(chain, 1)
                    dve.wait_ge(chain, at)
                at = at + 1
                dve.bn_stats(stat, rows).then_inc(chain, 1)
                wait_alone(dve, passed, (chain, at))
                dve.bn_aggr(mean_var, stat).then_inc(var_done, 1)
                dve.wait_ge(root_done, root_at)
                link(dve.reciprocal(rstd, rstd))
                link(dve.tensor_scalar(rows, rows, mean_var[:, 0:1], rstd, op0=ALU.subtract, op1=ALU.mult))
                link(dve.tensor_tensor(rows, rows, vec[:, gain, :], ALU.mult))
                dve.tensor_tensor(out, rows, vec[:, shift, :], ALU.add).then_inc(sem_done, 1)

            CH1 = 6

            def chain_at(g, kind, t):
                base = row_at(g, kind, t)
                return base * CH1

            def attn_rows(g, b):
                dve.wait_ge(x_in, (g + 1) * 16)
                for t in range(TG):
                    at = chain_at(g, 0, t)
                    dve.tensor_tensor(xr[:, t, :], xr[:, t, :], vec[:, BO, :], ALU.add).then_inc(chain, 1)
                    dve.wait_ge(chain, at + 1)
                    dve.wait_ge(row_done, row_at(g, 0, t) + 1)
                    dve.tensor_tensor(xr[:, t, :], xr[:, t, :], row_ps[:, t % 2, :], ALU.add).then_inc(row_read, 1)
                    dve.wait_ge(row_read, row_at(g, 0, t) + 1)
                    if t == 0 and not (isinstance(g, int) and g < 2):
                        dve.wait_ge(tr_done, (g - 1) * 2 * CD)
                    norm(at + 1, xr[:, t, :], h1[b][:, t, :], bn[:, t, :], mv[:, t, :], rs[:, t, :], G1, BE1, h1_done, row_at(g, 0, t) + 1)
                    dve.wait_ge(h1_done, g * TG + t + 1)
                    dve.sem_inc(chain, 1)

            def out_rows(g, b):
                for t in range(TG):
                    at = chain_at(g, 1, t)
                    dve.tensor_tensor(h1[b][:, t, :], h1[b][:, t, :], vec[:, B2, :], ALU.add).then_inc(chain, 1)
                    dve.wait_ge(chain, at + 1)
                    dve.wait_ge(row_done, row_at(g, 1, t) + 1)
                    dve.tensor_tensor(h1[b][:, t, :], h1[b][:, t, :], row_ps[:, 2 + t % 2, :], ALU.add).then_inc(row_read, 1)
                    dve.wait_ge(row_read, row_at(g, 1, t) + 1)
                    if t == 0 and not first(g):
                        dve.wait_ge(stored, g * 16)
                    norm(at + 1, h1[b][:, t, :], ob[:, t, :], bn2[:, t, :], mv2[:, t, :], rs2[:, t, :], G2, BE2, ob_done, row_at(g, 1, t) + 1)
                    dve.sem_inc(chain, 1)

            attn_rows(0, 0)
            with dve.Fori(0, NG // 2 - 1) as pair:
                g2 = pair * 2
                for b in range(2):
                    attn_rows(g2 + b + 1, 1 - b)
                    out_rows(g2 + b, b)
            attn_rows(NG - 1, 1)
            out_rows(NG - 2, 0)
            out_rows(NG - 1, 1)


def layer(nc, a):
    dram = lambda name, shape, dt=F32: nc.dram_tensor(name, shape, dt, kind="Internal").ap()
    q_tab = dram("q_tab", [N, D])
    kv_tab = dram("kv_tab", [N, 2 * D])
    rec_tab = dram("rec_tab", [T * REC_TILE + P, REC], I32)
    ctx_rows = dram("ctx_rows", [N, D])
    with (nc.sbuf_tensor("it_index", [P, 2, IMAX], I32) as it_index,
          nc.sbuf_tensor("it_merge", [P, 2, IMAX], F32) as it_merge,
          nc.sbuf_tensor("rounds", [P, 2], I32) as rounds):
        project_and_list(nc, a, q_tab, kv_tab, rec_tab, it_index, it_merge, rounds)
        attend(nc, a["adj_tab"], q_tab, kv_tab, rec_tab, it_index, it_merge, rounds, a["bk"], ctx_rows, a["ident"], a["iota"])
    feed_forward(nc, a["x"], ctx_rows, a["woT"], a["w1T"], a["w2T"], a["bv"], a["bo"], a["b1"], a["b2"], a["g1"], a["be1"],
                 a["g2"], a["be2"], a["ident"], a["out"])


def constants():
    p = np.arange(P)
    t = np.arange(T)
    own = p[:, None] * B // P == t[None, :]
    return {
        "ident": np.eye(P, dtype=np.float32),
        "iota": np.tile(np.arange(P, dtype=np.float32), (P, 1)),
        "iota_item": np.tile(np.arange(IMAX, dtype=np.float32), (P, 1)),
        "below": (p[:, None] < p[None, :]).astype(np.float32),
        "own": own.astype(np.float32),
        "column": p[:, None].astype(np.float32),
        "slot": np.arange(N).reshape(HI, LO).astype(np.float32),
        "number": (np.arange(N) - N // 2).reshape(P, B).astype(np.float16),
        "tile_c": np.tile(np.stack([t * N - 1, T * N - t * N + 1, -1 - t * P]).astype(np.float32), (HI, 1, 1)),
    }


def kernel(**inputs):
    import concourse.bacc as bacc
    from concourse.bass_utils import run_bass_kernel_spmd
    from concourse import mybir as _mybir

    given = {k.removeprefix("L0_gnn_"): np.asarray(v) for k, v in inputs.items()}
    names = {"bq": "bq", "bk": "bk", "bv": "bv", "bo": "bo", "b1": "b1", "b2": "b2",
             "g1": "ln1_g", "be1": "ln1_b", "g2": "ln2_g", "be2": "ln2_b"}
    arrays = {k: np.ascontiguousarray(given[v]) for k, v in names.items()}
    for k, v in {"wqT": "Wq", "wkT": "Wk", "wvT": "Wv", "woT": "Wo", "w1T": "W1", "w2T": "W2", "xT": "x"}.items():
        arrays[k] = np.ascontiguousarray(given[v].T)
    for k in ("bq", "bk", "bv", "b1"):
        arrays[k] = np.ascontiguousarray(arrays[k].reshape(-1, P).T)
    arrays["x"] = np.ascontiguousarray(given["x"])
    adj = given["adj"].reshape(T, P, N).transpose(0, 2, 1).reshape(T * N, P)
    arrays["adj_tab"] = np.concatenate([adj, np.zeros((1, P), adj.dtype)])
    arrays |= constants()

    nc = bacc.Bacc("TRN2", target_bir_lowering=False, num_devices=1)
    args = {k: nc.dram_tensor(f"in_{k}", v.shape, _mybir.dt.from_np(v.dtype), kind="ExternalInput").ap()
            for k, v in arrays.items()}
    args["out"] = nc.dram_tensor("out_rows", [N, D], F32, kind="ExternalOutput").ap()
    layer(nc, args)
    r = run_bass_kernel_spmd(nc, [{f"in_{k}": v for k, v in arrays.items()}], core_ids=[0])
    return r.results[0]["out_rows"]
```

```python
import numpy as np
import concourse.bass as bass
from concourse import mybir
from contextlib import ExitStack

F32 = mybir.dt.float32
F32R = mybir.dt.float32r
BF16 = mybir.dt.bfloat16
F16 = mybir.dt.float16
I32 = mybir.dt.int32
U32 = mybir.dt.uint32
ALU = mybir.AluOpType
ACT = mybir.ActivationFunctionType
AX = mybir.AxisListType

P = 128
N = 4096
D = 512
H = 8
DK = D // H
F = 2048
EPS = 1e-5
SCALE = DK ** -0.5
CD = D // P
CF = F // P
T = N // P
G = 512
NG = N // G
TG = G // P
RF = 256
NF = N // RF
TF = RF // P
CK = 2
KEYS = CK * P
MASKED = -8e9
RESET = 1e30
BANK = 512
HB = BANK // KEYS
U = H // HB
NB = 4
ROUNDS = (T * (N // KEYS) + NB - 1) // NB
IMAX = (ROUNDS + 2) * NB
B = N // P
LO = 64
HI = N // LO
REC_K, REC_ADJ, REC_REL, REC = 0, CK, 2 * CK, 3 * CK
REC_TILE = N // CK


def wait_alone(engine, passed, *waits):
    for semaphore, value in waits:
        engine.wait_ge(semaphore, value)
        engine.sem_inc(passed, 1)


def project_and_list(nc, a, q_tab, kv_tab, rec_tab, it_index, it_reset, rounds):
    with ExitStack() as ctx:
        sb = lambda name, shape, dt=F32: ctx.enter_context(nc.sbuf_tensor(f"qkv_{name}", shape, dt))
        sem = lambda name: ctx.enter_context(nc.semaphore(f"qkv_{name}"))
        ps = lambda name, shape: ctx.enter_context(nc.psum_tensor(f"qkv_{name}", shape, F32))
        w = [sb(f"w_{n}", [P, CD, D]) for n in "qkv"]
        bq = sb("bq", [P, CD])
        x = [sb(f"x_{b}", [P, CD, G]) for b in range(2)]
        q = [sb(f"q_{b}", [P, TG, CD, P]) for b in range(2)]
        kv = [sb(f"kv_{b}", [P, TG, 2, D]) for b in range(2)]
        HALF = B // 2
        adj = sb("adj", [P, 4, HALF, P], I32)
        own = sb("own", [P, T])
        below = sb("below", [P, P])
        iota = sb("iota", [P, P])
        column = sb("column", [P, 1])
        iota_item = sb("iota_item", [P, IMAX])
        tile_c = sb("tile_c", [HI, 3, T])
        slot = sb("slot", [HI, LO])
        number = sb("number", [P, B], F16)
        ones = sb("ones", [P, IMAX])
        inside = sb("inside", [P, TG, B])
        found = sb("found", [P, T * B])
        red = sb("red", [P, 4, HALF])
        cnt = sb("cnt", [P, TG])
        before = sb("before", [P, TG])
        total = sb("total", [P, T])
        place = sb("place", [P, TG, B])
        place_i = sb("place_i", [P, TG, B], I32)
        part_i = sb("part_i", [P, TG, B], I32)
        hi = sb("hi", [P, T * B])
        lo = sb("lo", [P, T * B])
        oh_hi = [sb(f"oh_hi_{b}", [P, B, HI], F16) for b in range(2)]
        oh_lo = [sb(f"oh_lo_{b}", [P, B, LO], F16) for b in range(2)]
        oh_n = [sb(f"oh_n_{b}", [P, B, LO], F16) for b in range(2)]
        node = sb("node", [HI, T, LO])
        rec = sb("rec", [HI, TG, LO // CK, REC], I32)
        r0 = sb("r0", [HI, TG, LO])
        r1 = sb("r1", [HI, TG, LO])
        adj_flat = adj[:, :, :, :].rearrange("p n b q -> p (n b q)")
        it_tile, it_same, it_nth, it_t0, it_t1, past = (
            adj_flat.bitcast(F32)[:, n * IMAX:(n + 1) * IMAX] for n in range(6))
        later = sb("later", [T, T])
        mine = sb("mine", [T, 2])
        pad = sb("pad", [P, REC], I32)
        gi = sb("gi", [P, T], I32)
        gf = sb("gf", [P, T])
        cum = sb("cum", [P, T])
        rnd = sb("rnd", [P, IMAX // NB])
        q_ps = ps("q_ps", [P, 2, G])
        kv_ps = ps("kv_ps", [P, 4, D])
        l_ps = ps("l_ps", [P, 2, 512])
        BASE = 256
        w_in, c_in = sem("w_in"), sem("c_in")
        x_in = [sem(f"x_in_{b}") for b in range(2)]
        q_out = [sem(f"q_out_{b}") for b in range(2)]
        kv_out = [sem(f"kv_out_{b}") for b in range(2)]
        q_sum, q_done = sem("q_sum"), sem("q_done")
        kv_sum, kv_done = sem("kv_sum"), sem("kv_done")
        adj_in = [sem(f"adj_in_{b}") for b in range(4)]
        red_done = sem("red_done")
        found_done = sem("found_done")
        cnt_done = sem("cnt_done")
        base_done = sem("base_done")
        hi_done, lo_done = sem("hi_done"), sem("lo_done")
        number_done = sem("number_done")
        list_sum, list_done = sem("list_sum"), sem("list_done")
        chain = sem("chain")
        past_done, tile_sum = sem("past_done"), sem("tile_sum")
        placed = sem("placed")
        rec_done, rec_out = sem("rec_done"), sem("rec_out")
        passed = sem("passed")
        block = ctx.enter_context(nc.Block())

        @block.sync
        def _(sp):
            def load(t, half, n):
                src = a["adj_tab"][bass.ds(t * N, N), :].rearrange("(p b) q -> p b q", b=B)
                sp.dma_start(adj[:, n, :, :], src[:, half * HALF:(half + 1) * HALF, :]).then_inc(adj_in[n], 16)

            for n, name in enumerate(("wqT", "wkT", "wvT")):
                sp.dma_start(w[n][:, :, :], a[name].rearrange("(c p) o -> p c o", p=P)).then_inc(w_in, 16)
            sp.dma_start(bq[:, :], a["bq"]).then_inc(w_in, 16)
            for n in range(4):
                load(n // 2, n % 2, n)

            def loads(batch, tiles=range(TG)):
                for i in tiles:
                    for half in range(2):
                        t = batch * TG + i
                        wait_alone(sp, passed, (red_done, t * 2 + half - 3))
                        load(t, half, i % 2 * 2 + half)

            def store_rows(batch):
                wait_alone(sp, passed, (rec_done, batch + 1))
                sp.dma_start(rec_tab[0:T * REC_TILE, :].rearrange("(t h r) w -> h t (r w)", h=HI, r=LO // CK)[:, bass.ds(batch * TG, TG), :],
                             rec[:, :, :, :].rearrange("h t r w -> h t (r w)")).then_inc(rec_out, 16)

            LATE = 4
            loads(0, range(2, TG))
            with sp.Fori(1, LATE) as batch:
                loads(batch)
            with sp.Fori(LATE, NG) as batch:
                store_rows(batch - LATE)
                loads(batch)
            for batch in range(NG - LATE, NG):
                store_rows(batch)
            sp.wait_ge(rec_done, NG + 1)
            sp.dma_start(rec_tab[T * REC_TILE:T * REC_TILE + P, :], pad[:, :]).then_inc(rec_out, 16)
            sp.wait_ge(rec_out, 16 * (NG + 1))
            for b in range(2):
                sp.wait_ge(q_out[b], 16 * NG // 2)
                sp.wait_ge(kv_out[b], 16 * NG // 2)

        @block.gpsimd
        def _(pool):
            def load(g, b):
                pool.dma_start(x[b][:, :, :], a["xT"][:, bass.ds(g * G, G)].rearrange("(c p) n -> p c n", p=P))\
                    .then_inc(x_in[b], 16)

            def store(g, b):
                wait_alone(pool, passed, (q_done, (g + 1) * CD))
                pool.dma_start(q_tab[bass.ds(g * G, G), :].rearrange("(t p) f -> p t f", p=P),
                               q[b][:, :, :, :].rearrange("p t c q -> p t (c q)")).then_inc(q_out[b], 16)
                wait_alone(pool, passed, (kv_done, (g + 1) * 2 * TG))
                pool.dma_start(kv_tab[bass.ds(g * G, G), :].rearrange("(t p) f -> p t f", p=P),
                               kv[b][:, :, :, :].rearrange("p t c q -> p t (c q)")).then_inc(kv_out[b], 16)

            def numbers(batch):
                for i in range(TG):
                    wait_alone(pool, passed, (lo_done, batch * TG + i + 1))
                    pool.tensor_tensor(oh_n[i % 2][:, :, :], oh_lo[i % 2][:, :, :],
                                       number[:, :].unsqueeze(2).broadcast_to([P, B, LO]), ALU.mult).then_inc(number_done, 1)

            load(0, 0)
            load(1, 1)
            for dst, name in ((own, "own"), (below, "below"), (iota, "iota"), (column, "column"),
                              (iota_item, "iota_item"), (slot, "slot"), (number, "number")):
                pool.dma_start(dst[:, :], a[name]).then_inc(c_in, 16)
            pool.dma_start(tile_c[:, :, :], a["tile_c"]).then_inc(c_in, 16)
            store(0, 0)
            load(2, 0)
            with pool.Fori(0, NG // 2 - 2) as pair:
                for b in range(2):
                    numbers(pair * 2 + b)
                    store(pair * 2 + b + 1, 1 - b)
                    load(pair * 2 + b + 3, 1 - b)
            numbers(NG - 4)
            store(NG - 3, 1)
            load(NG - 1, 1)
            numbers(NG - 3)
            store(NG - 2, 0)
            numbers(NG - 2)
            store(NG - 1, 1)
            numbers(NG - 1)

        @block.tensor
        def _(pe):
            pe.wait_ge(w_in, 16 * 4)

            def lists(batch, i):
                t, b = batch * TG + i, i % 2
                pe.wait_ge(hi_done, t + 1)
                pe.wait_ge(number_done, t + 1)
                if not (isinstance(t, int) and t < 2):
                    pe.wait_ge(list_done, t - 1)
                for n in range(B):
                    mm = pe.matmul(l_ps[0:HI, b, 0:LO], oh_hi[b][:, n, :], oh_n[b][:, n, :], start=n == 0, stop=n == B - 1)
                mm.then_inc(list_sum, 1)

            def group(g, b):
                first = isinstance(g, int) and g == 0
                pe.wait_ge(x_in[b], g * 8 + 16 - 8 * b)
                for c in range(CD):
                    if not (first and c < 2):
                        pe.wait_ge(q_done, g * CD + c - 1)
                    for i in range(CD):
                        mm = pe.matmul(q_ps[:, c % 2, :], w[0][:, i, c * P:(c + 1) * P], x[b][:, i, :],
                                       start=i == 0, stop=i == CD - 1)
                    mm.then_inc(q_sum, 1)
                for t in range(TG):
                    for n in range(2):
                        at = 2 * t + n
                        if at >= 4 or not first:
                            pe.wait_ge(kv_done, g * 2 * TG + at - 3)
                        for i in range(CD):
                            mm = pe.matmul(kv_ps[:, at % 4, :], x[b][:, i, t * P:(t + 1) * P], w[1 + n][:, i, :],
                                           start=i == 0, stop=i == CD - 1)
                        mm.then_inc(kv_sum, 1)
                    if not first:
                        lists(g - 1, t)
                pe.wait_ge(cnt_done, g + 1)
                if not first:
                    pe.wait_ge(list_done, g * TG)
                pe.matmul(l_ps[:, 0, BASE:BASE + TG], below[:, :], cnt[:, :], start=True, stop=True)
                pe.matmul(l_ps[:, 0, BASE + TG:BASE + 2 * TG], ones[:, 0:P], cnt[:, :], start=True, stop=True).then_inc(base_done, 1)

            group(0, 0)
            group(1, 1)
            with pe.Fori(1, NG // 2) as pair:
                for b in range(2):
                    group(pair * 2 + b, b)
            for t in range(TG):
                lists(NG - 1, t)
            pe.wait_ge(past_done, 1)
            pe.matmul(l_ps[:, 0, :], ones[0:T, 0:P], past[0:T, 0:BANK], start=True, stop=True)
            pe.matmul(l_ps[:, 1, 0:IMAX - BANK], ones[0:T, 0:P], past[0:T, BANK:IMAX], start=True, stop=True).then_inc(tile_sum, 1)

        @block.scalar
        def _(act):
            act.wait_ge(w_in, 16 * 4)

            def lists(batch, i):
                t = batch * TG + i
                act.wait_ge(list_sum, t + 1)
                act.sem_inc(passed, 1)
                act.activation(node[:, bass.ds(t, 1), :], l_ps[0:HI, i % 2, 0:LO].unsqueeze(1), ACT.Copy).then_inc(list_done, 1)

            def group(g, b):
                early = isinstance(g, int) and g < 2
                if not early:
                    act.wait_ge(q_out[b], g * 8 - 8 * b)
                for c in range(CD):
                    act.wait_ge(q_sum, g * CD + c + 1)
                    act.activation(q[b][:, :, c, :], q_ps[:, c % 2, :].rearrange("p (t q) -> p t q", q=P),
                                   ACT.Identity, bias=bq[:, c:c + 1]).then_inc(q_done, 1)
                if not early:
                    act.wait_ge(kv_out[b], g * 8 - 8 * b)
                for t in range(TG):
                    for n in range(2):
                        at = 2 * t + n
                        act.wait_ge(kv_sum, g * 2 * TG + at + 1)
                        act.activation(kv[b][:, t, n, :], kv_ps[:, at % 4, :], ACT.Copy).then_inc(kv_done, 1)
                    if not (isinstance(g, int) and g == 0):
                        lists(g - 1, t)

            group(0, 0)
            group(1, 1)
            with act.Fori(1, NG // 2) as pair:
                for b in range(2):
                    group(pair * 2 + b, b)
            for t in range(TG):
                lists(NG - 1, t)

        @block.vector
        def _(dve):
            at = 0

            def link(ins):
                nonlocal at
                at = at + 1
                ins.then_inc(chain, 1)
                dve.wait_ge(chain, at)

            dve.wait_ge(c_in, 16 * 8)
            link(dve.memset(ones[:, :], 1.0))
            link(dve.memset(inside[:, :, :], 1.0))
            link(dve.memset(inside[:, :, 0:1], 0.0))
            batch_from = at
            LINKS, ROW_LINKS = 9, 8
            behind = 2
            first_link = lambda n: n * LINKS + ((n - behind) * ROW_LINKS if not isinstance(n, int) or n > behind else 0) + batch_from

            def flags(t, n, seen):
                dve.wait_ge(adj_in[n], seen * 16 + 16)
                dve.tensor_reduce(red[:, n, :], adj[:, n, :, :], AX.X, ALU.max, apply_absolute_value=True).then_inc(red_done, 1)
                dve.wait_ge(red_done, t * 2 + n % 2 + 1)
                dve.tensor_scalar(found[:, bass.ds(t * B + n % 2 * HALF, HALF)], red[:, n, :], 0.0, own[:, bass.ds(t, 1)],
                                  op0=ALU.not_equal, op1=ALU.max).then_inc(found_done, 1)

            def one_hot(batch, i):
                t, b = batch * TG + i, i % 2
                if not (isinstance(t, int) and t < 2):
                    dve.wait_ge(list_sum, t - 1)
                wide = lambda ap: ap[:, bass.ds(t * B, B)].unsqueeze(2).broadcast_to([P, B, LO])
                counted = iota[:, 0:LO].unsqueeze(1).broadcast_to([P, B, LO])
                dve.tensor_tensor(oh_lo[b][:, :, :], wide(lo), counted, ALU.is_equal).then_inc(lo_done, 1)
                dve.tensor_tensor(oh_hi[b][:, :, :], wide(hi), counted, ALU.is_equal).then_inc(hi_done, 1)

            def places(n):
                nonlocal at
                at = first_link(n)
                marks = found[:, bass.ds(n * (TG * B), TG * B)].rearrange("p (t b) -> p t b", b=B)
                flat = lambda ap: ap[:, :, :].rearrange("p t b -> p (t b)")
                dve.wait_ge(found_done, n * (2 * TG) + 2 * TG)
                dve.tensor_reduce(cnt[:, :], marks, AX.X, ALU.add).then_inc(cnt_done, 1)
                link(dve.tensor_tensor_scan(flat(place), flat(inside), found[:, bass.ds(n * (TG * B), TG * B)], 0.0,
                                            op0=ALU.mult, op1=ALU.add))
                dve.wait_ge(base_done, n + 1)
                link(dve.tensor_copy(before[:, :], l_ps[:, 0, BASE:BASE + TG]))
                link(dve.tensor_copy(total[:, bass.ds(n * TG, TG)], l_ps[:, 0, BASE + TG:BASE + 2 * TG]))
                link(dve.tensor_tensor(place[:, :, :], place[:, :, :], before[:, :].unsqueeze(2).broadcast_to([P, TG, B]), ALU.add))
                link(dve.tensor_tensor(place[:, :, :], place[:, :, :], marks, ALU.mult))
                link(dve.tensor_scalar(place_i[:, :, :], place[:, :, :], -1.0, None, op0=ALU.add))
                link(dve.tensor_scalar(part_i[:, :, :], place_i[:, :, :], LO.bit_length() - 1, None, op0=ALU.arith_shift_right))
                dve.tensor_copy(hi[:, bass.ds(n * (TG * B), TG * B)], flat(part_i)).then_inc(chain, 1)
                link(dve.tensor_scalar(place_i[:, :, :], place_i[:, :, :], LO - 1, None, op0=ALU.bitwise_and))
                at = at + 1
                dve.wait_ge(chain, at)
                dve.tensor_copy(lo[:, bass.ds(n * (TG * B), TG * B)], flat(place_i)).then_inc(placed, 1)
                dve.wait_ge(placed, n + 1)

            def rows(n):
                tiles = bass.ds(n * TG, TG)
                dve.wait_ge(list_done, (n + 1) * TG)
                if not (isinstance(n, int) and n == 0):
                    dve.wait_ge(rec_out, n * 16)
                nd = node[:, tiles, :]
                col = lambda ap: ap.unsqueeze(2).broadcast_to([HI, TG, LO])
                part = lambda c: rec[:, :, :, c:c + CK]
                r4 = lambda ap: ap.rearrange("h t (r c) -> h t r c", c=CK)
                z0, z1 = r0[:, :, :], r1[:, :, :]
                link(dve.tensor_tensor(z0, slot[:, :].unsqueeze(1).broadcast_to([HI, TG, LO]), col(total[0:HI, tiles]), ALU.is_lt))
                link(dve.scalar_tensor_tensor(nd, nd, float(N // 2 + 1), z0, op0=ALU.add, op1=ALU.mult))
                link(dve.tensor_scalar(part(REC_K), r4(nd), -1.0, 0.0, op0=ALU.add, op1=ALU.max))
                link(dve.tensor_scalar(z0, nd, 0.0, None, op0=ALU.is_equal))
                link(dve.tensor_tensor(z0, z0, col(tile_c[:, 1, tiles]), ALU.mult))
                link(dve.tensor_tensor(z1, nd, col(tile_c[:, 0, tiles]), ALU.add))
                link(dve.tensor_tensor(part(REC_ADJ), r4(z0), r4(z1), ALU.add))
                link(dve.tensor_tensor(part(REC_REL).bitcast(F32), r4(nd), r4(col(tile_c[:, 2, tiles])), ALU.add))
                dve.sem_inc(rec_done, 1)

            for i in range(TG):
                for half in range(2):
                    flags(i, i % 2 * 2 + half, i // 2)
            places(0)

            def batch(n):
                for i in range(TG):
                    for half in range(2):
                        flags(n * TG + i, i % 2 * 2 + half, n * (TG // 2) + i // 2)
                    one_hot(n - 1, i)
                places(n)
                if not isinstance(n, int) or n >= behind:
                    rows(n - behind)

            for n in range(1, behind + 1):
                batch(n)
            with dve.Fori(behind + 1, NG) as n:
                batch(n)
            at = first_link(NG)
            for i in range(TG):
                one_hot(NG - 1, i)

            link(dve.tensor_scalar(gi[:, :], total[:, :], float(KEYS - 1), None, op0=ALU.add))
            link(dve.tensor_scalar(gi[:, :], gi[:, :], KEYS.bit_length() - 1, None, op0=ALU.arith_shift_right))
            link(dve.tensor_copy(gf[:, :], gi[:, :]))
            link(dve.tensor_tensor_scan(cum[:, :], ones[:, 0:T], gf[:, :], 0.0, op0=ALU.mult, op1=ALU.add))
            link(dve.tensor_tensor(later[:, :], gf[0:T, :], below[0:T, 0:T], ALU.mult))
            link(dve.tensor_reduce(mine[:, 0:1], later[:, :], AX.X, ALU.add))
            link(dve.tensor_tensor(mine[:, 1:2], cum[0:T, T - 1:T], mine[:, 0:1], ALU.subtract))
            dve.wait_ge(list_done, T)
            link(dve.tensor_scalar(past[0:T, :], iota_item[0:T, :], mine[:, 1:2], None, op0=ALU.is_ge))
            dve.sem_inc(past_done, 1)
            dve.wait_ge(tile_sum, 1)
            link(dve.tensor_copy(it_tile[:, 0:BANK], l_ps[:, 0, :]))
            link(dve.tensor_copy(it_tile[:, BANK:IMAX], l_ps[:, 1, 0:IMAX - BANK]))
            link(dve.memset(it_same, 0.0))
            link(dve.tensor_tensor(it_same[:, 1:IMAX], it_tile[:, 1:IMAX], it_tile[:, 0:IMAX - 1], ALU.is_equal))
            link(dve.tensor_tensor_scan(it_nth, ones[:, 0:IMAX], it_same, 0.0, op0=ALU.add, op1=ALU.mult))
            link(dve.tensor_scalar(it_t0, it_nth, float(P), None, op0=ALU.mult))
            link(dve.scalar_tensor_tensor(it_t0, it_tile, float(REC_TILE), it_t0, op0=ALU.mult, op1=ALU.add))
            link(dve.tensor_scalar(it_index[:, 0, :], it_t0, float(T * REC_TILE), column[:, 0:1], op0=ALU.min, op1=ALU.add))
            link(dve.tensor_scalar(it_t1, it_tile, float(T - 1), float(P), op0=ALU.min, op1=ALU.mult))
            link(dve.tensor_scalar(it_index[:, 1, :], it_t1, column[:, 0:1], None, op0=ALU.add))
            link(dve.scalar_tensor_tensor(it_t0, it_tile, T - 0.5, it_same, op0=ALU.is_gt, op1=ALU.max))
            link(dve.tensor_scalar(it_reset[:, :], it_t0, -1.0, RESET, op0=ALU.add, op1=ALU.mult))
            link(dve.tensor_scalar(rnd[:, :], iota_item[:, 0:IMAX:NB], cum[:, T - 1:T], None, op0=ALU.is_lt))
            link(dve.tensor_reduce(gf[:, 0:1], rnd[:, :], AX.X, ALU.add))
            link(dve.tensor_copy(rounds[:, 0:1], gf[:, 0:1]))
            link(dve.tensor_scalar(rounds[:, 1:2], gf[:, 0:1], -1.0, None, op0=ALU.add))
            link(dve.memset(pad[:, REC_K:REC_ADJ], 0))
            link(dve.memset(pad[:, REC_ADJ:REC_REL], T * N))
            link(dve.memset(pad[:, REC_REL:REC].bitcast(F32), -1.0))

            for n in range(NG - behind, NG):
                rows(n)
            dve.sem_inc(rec_done, 1)


def attend(nc, early, adj_tab, q_tab, kv_tab, rec_tab, it_index, it_reset, rounds, b_k, ctx_out, ident_in, iota_in):
    with ExitStack() as ctx:
        sb = lambda name, shape, dt=F32: ctx.enter_context(nc.sbuf_tensor(f"att_{name}", shape, dt))
        ring = lambda name, shape, dt=F32: [sb(f"{name}_{b}", shape, dt) for b in range(NB)]
        ps = lambda name, shape: ctx.enter_context(nc.psum_tensor(f"att_{name}", shape, F32))
        sem = lambda name: ctx.enter_context(nc.semaphore(f"att_{name}"))
        sems = lambda name: [sem(f"{name}_{b}") for b in range(NB)]
        ident = sb("ident", [P, P])
        iota = sb("iota", [P, P])
        bk = sb("bk", [P, CD])
        index = ring("index", [P, 2], I32)
        index_out = ring("index_out", [P, 1], I32)
        rec = ring("rec", [P, REC], I32)
        kv = ring("kv", [P, CK, 2 * D])
        adj = ring("adj", [P, CK, P], I32)
        qT = ring("qT", [P, CD, P])
        maskT = ring("maskT", [P, CK, P])
        mask = ring("mask", [P, KEYS])
        kT = ring("kT", [P, CD, KEYS])
        s = ring("s", [P, H, KEYS])
        pT = sb("pT", [P, 2, HB * CK, P])
        gmax = ring("gmax", [P, H])
        mrun = ring("mrun", [P, H])
        mdiff = ring("mdiff", [P, H])
        negm = ring("negm", [P, H])
        alpha = ring("alpha", [P, H])
        gsum = ring("gsum", [P, H])
        orun = ring("orun", [P, H, DK + 1])
        tr_ps = ps("tr_ps", [P, 2, BANK])
        s_ps = ps("s_ps", [P, 2, BANK])
        pT_ps = ps("pT_ps", [P, 2, BANK])
        o_ps = ps("o_ps", [P, 2, D])
        const_in, early_in = sem("const_in"), sem("early_in")
        rec_in, kv_in, adj_in, q_in = sems("rec_in"), sems("kv_in"), sems("adj_in"), sems("q_in")
        index_done = sem("index_done")
        out_index = sem("out_index")
        ctx_stored = sem("ctx_stored")
        maskT_done = sem("maskT_done")
        tr_done = sem("tr_done")
        tr_read = sem("tr_read")
        s_done = sem("s_done")
        s_read = sem("s_read")
        stat_done = sem("stat_done")
        alpha_done = sem("alpha_done")
        p_done = sem("p_done")
        pT_done = sem("pT_done")
        pT_read = sem("pT_read")
        pv_done = sem("pv_done")
        o_done = sem("o_done")
        init = sem("init")
        chain = sem("chain")
        passed = sem("passed")
        block = ctx.enter_context(nc.Block())
        HH, UH = H // 2, U // 2
        TR = 1 + CD // HB

        def heads(u):
            return [u // 2 * 2 * HB + u % 2 + 2 * j for j in range(HB)]

        class Item:

            def __init__(self, k, b):
                self.k, self.b = k + b // NB, b % NB
                self.i = self.k * NB + self.b
                self.first = isinstance(self.k, int) and self.k == 0
                self.uses = self.k * 16 + 16

            def ahead(self, n):
                return Item(self.k, self.b + n)

        def each_step(engine, step, count):
            for b in range(NB):
                step(Item(0, b))
            with engine.Fori(1, count) as k:
                for b in range(NB):
                    step(Item(k, b))

        @block.sync
        def _(sp):
            sp.dma_start(ident[:, :], ident_in).then_inc(const_in, 16)
            sp.dma_start(iota[:, :], iota_in).then_inc(const_in, 16)
            sp.dma_start(bk[:, :], b_k).then_inc(const_in, 16)
            sp.wait_ge(s_done, 1)
            for dst, src in early:
                sp.dma_start(dst, src).then_inc(early_in, 16)
            sp.wait_ge(early_in, 16 * len(early))

        @block.gpsimd
        def _(pool):
            count = pool.value_load(rounds[0:1, 0:1], min_val=2, max_val=ROUNDS)
            last = pool.value_load(rounds[0:1, 1:2], min_val=1, max_val=ROUNDS - 1)

            def gather(out, src, index):
                return pool.indirect_dma_start(out=out, out_offset=None, in_=src,
                                               in_offset=bass.IndirectOffsetOnAxis(ap=index.bitcast(U32), axis=0))

            def load_rec(it):
                if not it.first:
                    wait_alone(pool, passed,
                               (maskT_done, it.i - NB + 1),
                               (kv_in[it.b], it.k * (16 * CK)),
                               (q_in[it.b], it.k * 16))
                pool.tensor_copy(index[it.b][:, :], it_index[:, :, bass.ds(it.i, 1)].rearrange("p n i -> p (n i)"))\
                    .then_inc(index_done, 1)
                wait_alone(pool, passed, (index_done, it.i + 1))
                gather(rec[it.b][:, :], rec_tab, index[it.b][:, 0:1]).then_inc(rec_in[it.b], 16)

            def load_adj(it):
                wait_alone(pool, passed, (rec_in[it.b], it.uses))
                for c in range(CK):
                    gather(adj[it.b][:, c, :], adj_tab, rec[it.b][:, REC_ADJ + c:REC_ADJ + c + 1]).then_inc(adj_in[it.b], 16)

            def load(it):
                if not it.first:
                    wait_alone(pool, passed, (s_done, (it.i - NB + 1) * U))
                gather(qT[it.b][:, :, :].rearrange("p c q -> p (c q)"), q_tab, index[it.b][:, 1:2]).then_inc(q_in[it.b], 16)
                if not it.first:
                    wait_alone(pool, passed, (pv_done, (it.i - NB + 1) * U))
                for c in range(CK):
                    gather(kv[it.b][:, c, :], kv_tab, rec[it.b][:, REC_K + c:REC_K + c + 1]).then_inc(kv_in[it.b], 16)

            def store(it):
                if not (it.first and it.b == 0):
                    wait_alone(pool, passed, (ctx_stored, it.i * 16))
                pool.tensor_copy(index_out[it.b][:, :], it_index[:, 1, bass.ds(it.i, 1)]).then_inc(out_index, 1)
                wait_alone(pool, passed, (out_index, it.i + 1), (o_done, it.i + 1))
                pool.indirect_dma_start(out=ctx_out, out_offset=bass.IndirectOffsetOnAxis(ap=index_out[it.b][:, :].bitcast(U32), axis=0),
                                        in_=orun[it.b][:, :, :].rearrange("p h d -> p (h d)"), in_offset=None).then_inc(ctx_stored, 16)

            def step(it):
                load_rec(it.ahead(3))
                load(it.ahead(2))
                load_adj(it.ahead(3))
                if not (it.first and it.b == 0):
                    store(Item(it.k - 1 if it.b == 0 else it.k, NB - 1 if it.b == 0 else it.b - 1))

            for b in range(3):
                load_rec(Item(0, b))
            for b in range(3):
                load_adj(Item(0, b))
                if b < 2:
                    load(Item(0, b))
            each_step(pool, step, count)
            store(Item(last, NB - 1))
            wait_alone(pool, passed, (ctx_stored, count * (16 * NB)))
            for b in range(3):
                wait_alone(pool, passed, (rec_in[b], count * 16 + 16))
                wait_alone(pool, passed, (adj_in[b], (count + 1) * (16 * CK)))
                if b < 2:
                    wait_alone(pool, passed, (kv_in[b], (count + 1) * (16 * CK)), (q_in[b], count * 16 + 16))

        @block.tensor
        def _(pe):
            pe.wait_ge(const_in, 48)
            count = pe.value_load(rounds[0:1, 0:1], min_val=2, max_val=ROUNDS)

            def unless_first(it, before, value, semaphore):
                if not (it.first and it.b == 0 and before < 2):
                    pe.wait_ge(semaphore, value)

            def tr(it, n):
                if n == 0:
                    pe.wait_ge(maskT_done, it.i + 1)
                if n == 1:
                    pe.wait_ge(kv_in[it.b], it.uses * CK)
                if n == 0 and not (it.first and it.b == 0):
                    pe.wait_ge(tr_read, it.i * TR)
                if n:
                    unless_first(it, n, it.i * TR + n - 1, tr_read)
                for j in range(1 if n == 0 else HB):
                    at = ((n - 1) * HB + j) * P
                    for c in range(CK):
                        src = maskT[it.b][:, c, :] if n == 0 else kv[it.b][:, c, at:at + P]
                        mm = pe.transpose(tr_ps[:, n % 2, (j * CK + c) * P:(j * CK + c + 1) * P], src, ident[:, :])
                mm.then_inc(tr_done, 1)

            def scores(it, u):
                if u == 0:
                    pe.wait_ge(q_in[it.b], it.uses)
                pe.wait_ge(tr_read, it.i * TR + heads(u)[-1] // 2 // HB + 2)
                unless_first(it, u, it.i * U + u - 1, s_read)
                for j, h in enumerate(heads(u)):
                    rows = slice(h % 2 * DK, h % 2 * DK + DK)
                    mm = pe.matmul(s_ps[:, u % 2, j * KEYS:(j + 1) * KEYS], qT[it.b][rows, h // 2, :],
                                   kT[it.b][rows, h // 2, :], start=True, stop=True)
                mm.then_inc(s_done, 1)

            def probT(it, u):
                pe.wait_ge(p_done, it.i * U + u + 1)
                unless_first(it, u, it.i * U + u - 1, pT_read)
                for n in range(HB * CK):
                    h, c = heads(u)[n // CK], n % CK
                    mm = pe.transpose(pT_ps[:, u % 2, n * P:(n + 1) * P], s[it.b][:, h, c * P:(c + 1) * P], ident[:, :])
                mm.then_inc(pT_done, 1)

            def values(it, u):
                pe.wait_ge(pT_read, it.i * U + u + 1)
                if u == 0 and not (it.first and it.b < 2):
                    pe.wait_ge(o_done, it.i - 1)
                for n in range(HB * CK):
                    h, c = heads(u)[n // CK], n % CK
                    mm = pe.matmul(o_ps[:, it.b % 2, h * DK:(h + 1) * DK], pT[:, u % 2, n, :],
                                   kv[it.b][:, c, D + h * DK:D + (h + 1) * DK], start=c == 0, stop=c == CK - 1)
                mm.then_inc(pv_done, 1)

            def step(it):
                nxt = it.ahead(1)
                tr(nxt, 0)
                for n in range(U + 1):
                    if n + 1 < TR:
                        tr(nxt, n + 1)
                    if n < U:
                        probT(it, n)
                    if n:
                        scores(nxt, n - 1)
                        values(it, n - 1)

            for n in range(TR):
                tr(Item(0, 0), n)
            for u in range(U):
                scores(Item(0, 0), u)
            each_step(pe, step, count)

        @block.scalar
        def _(act):
            act.wait_ge(const_in, 48)
            count = act.value_load(rounds[0:1, 0:1], min_val=2, max_val=ROUNDS)

            def tr(it, n):
                act.wait_ge(tr_done, it.i * TR + n + 1)
                if n == 0 and not it.first:
                    act.wait_ge(s_read, (it.i - NB + 1) * U)
                if n == 1 and not it.first:
                    act.wait_ge(s_done, (it.i - NB + 1) * U)
                if n == 0:
                    act.activation(mask[it.b][:, :], tr_ps[:, 0, 0:KEYS], ACT.Copy).then_inc(tr_read, 1)
                    return
                for j in range(HB):
                    c = (n - 1) * HB + j
                    ins = act.activation(kT[it.b][:, c, :], tr_ps[:, n % 2, j * KEYS:(j + 1) * KEYS], ACT.Identity, bias=bk[:, c:c + 1])
                ins.then_inc(tr_read, 1)

            def alphas(it, half):
                hs = slice(HH * half, HH * half + HH)
                act.wait_ge(stat_done, it.i * 2 + half + 1)
                if half == 0 and not it.first:
                    act.wait_ge(o_done, it.i - NB + 1)
                act.activation(alpha[it.b][:, hs], mdiff[it.b][:, hs], ACT.Exp, scale=SCALE).then_inc(alpha_done, 1)

            def probs(it, u):
                if u % UH == 0:
                    alphas(it, u // UH)
                for h in heads(u):
                    ins = act.activation(s[it.b][:, h, :], s[it.b][:, h, :], ACT.Exp, bias=negm[it.b][:, h:h + 1], scale=SCALE,
                                         accum_out=gsum[it.b][:, h:h + 1])
                ins.then_inc(p_done, 1)

            def probT(it, u):
                act.wait_ge(pT_done, it.i * U + u + 1)
                if not (it.first and it.b == 0 and u < 2):
                    act.wait_ge(pv_done, it.i * U + u - 1)
                act.activation(pT[:, u % 2, :, :].rearrange("p c q -> p (c q)"), pT_ps[:, u % 2, :], ACT.Copy)\
                   .then_inc(pT_read, 1)

            def step(it):
                nxt = it.ahead(1)
                tr(nxt, 0)
                for n in range(U + 1):
                    if n + 1 < TR:
                        tr(nxt, n + 1)
                    if n < U:
                        probT(it, n)
                    if n < UH:
                        probs(it, UH + n)
                    if n > UH:
                        probs(nxt, n - UH - 1)

            for n in range(TR):
                tr(Item(0, 0), n)
            for u in range(UH):
                probs(Item(0, 0), u)
            each_step(act, step, count)

        @block.vector
        def _(dve):
            dve.memset(mrun[NB - 1][:, :], 0.0).then_inc(init, 1)
            dve.memset(orun[NB - 1][:, :, :], 0.0).then_inc(init, 1)
            dve.wait_ge(init, 2)
            dve.wait_ge(const_in, 48)
            count = dve.value_load(rounds[0:1, 0:1], min_val=2, max_val=ROUNDS)
            STAT, MASK, MERGE = 3, CK, 1
            PER = 2 * STAT + MASK + MERGE
            AHEAD = 2 * MASK + 2 * STAT

            def link(ins, at):
                ins.then_inc(chain, 1)
                dve.wait_ge(chain, at)

            def masks(it, at):
                dve.wait_ge(rec_in[it.b], it.uses)
                dve.wait_ge(adj_in[it.b], it.uses * CK)
                if not it.first:
                    dve.wait_ge(tr_done, (it.i - NB) * TR + 1)
                for c in range(CK):
                    dve.scalar_tensor_tensor(maskT[it.b][:, c, :], iota[:, :], rec[it.b][:, REC_REL + c:REC_REL + c + 1].bitcast(F32),
                                             adj[it.b][:, c, :], op0=ALU.is_equal, op1=ALU.add).then_inc(chain, 1)
                dve.wait_ge(chain, at + CK)
                dve.tensor_scalar(maskT[it.b][:, :, :], maskT[it.b][:, :, :], 0.0, MASKED, op0=ALU.is_equal, op1=ALU.mult)\
                   .then_inc(maskT_done, 1)

            def scores(it, u):
                if u == 0:
                    dve.wait_ge(tr_read, it.i * TR + 1)
                    if not it.first:
                        dve.wait_ge(pT_done, (it.i - NB + 1) * U)
                wait_alone(dve, passed, (s_done, it.i * U + u + 1))
                for j, h in enumerate(heads(u)):
                    ins = dve.tensor_tensor_reduce(out=s[it.b][:, h, :], in0=s_ps[:, u % 2, j * KEYS:(j + 1) * KEYS], in1=mask[it.b][:, :],
                                                   scale=1.0, scalar=-3e38, op0=ALU.add, op1=ALU.max,
                                                   accum_out=gmax[it.b][:, h:h + 1])
                ins.then_inc(s_read, 1)

            def stats(it, half, at):
                hs = slice(HH * half, HH * half + HH)
                old, new = mrun[(it.b - 1) % NB][:, hs], mrun[it.b][:, hs]
                reset = it_reset[:, bass.ds(it.i, 1)]
                dve.wait_ge(s_read, it.i * U + UH * half + UH)
                if half == 0 and not it.first:
                    dve.wait_ge(p_done, (it.i - NB + 1) * U)
                link(dve.scalar_tensor_tensor(new, old, reset, gmax[it.b][:, hs], op0=ALU.add, op1=ALU.max), at + 1)
                dve.scalar_tensor_tensor(mdiff[it.b][:, hs], old, reset, new, op0=ALU.add, op1=ALU.subtract).then_inc(chain, 1)
                link(dve.tensor_scalar(negm[it.b][:, hs], new, -SCALE, None, op0=ALU.mult), at + 3)
                dve.sem_inc(stat_done, 1)

            def merge(it, at):
                old, new = orun[(it.b - 1) % NB], orun[it.b]
                dve.wait_ge(alpha_done, it.i * 2 + 2)
                if not it.first:
                    dve.wait_ge(ctx_stored, (it.i - NB + 1) * 16)
                link(dve.tensor_tensor(new[:, :, :], old[:, :, :], alpha[it.b][:, :].unsqueeze(2).broadcast_to([P, H, DK + 1]), ALU.mult), at + 1)
                dve.wait_ge(p_done, (it.i + 1) * U)
                dve.tensor_tensor(new[:, :, DK:DK + 1], new[:, :, DK:DK + 1], gsum[it.b][:, :].unsqueeze(2), ALU.add)
                dve.wait_ge(pv_done, (it.i + 1) * U)
                dve.tensor_tensor(new[:, :, 0:DK], new[:, :, 0:DK], o_ps[:, it.b % 2, :].rearrange("p (h d) -> p h d", d=DK), ALU.add)\
                   .then_inc(o_done, 1)
                dve.wait_ge(o_done, it.i + 1)

            def step(it):
                nxt, at = it.ahead(1), it.i * PER + AHEAD
                scores(nxt, 0)
                masks(it.ahead(2), at)
                for u in range(1, UH):
                    scores(nxt, u)
                stats(nxt, 0, at + MASK)
                for u in range(UH, U):
                    scores(nxt, u)
                stats(nxt, 1, at + MASK + STAT)
                merge(it, at + MASK + 2 * STAT)

            masks(Item(0, 0), 0)
            masks(Item(0, 1), MASK)
            for u in range(U):
                scores(Item(0, 0), u)
            for half in range(2):
                stats(Item(0, 0), half, 2 * MASK + half * STAT)
            each_step(dve, step, count)


def feed_forward(nc, x_rows, ctx_rows, weights, rest, vec, scratch, b_v, b_1, ident_in, out):
    with ExitStack() as ctx:
        sb = lambda name, shape, dt=F32: ctx.enter_context(nc.sbuf_tensor(f"ff_{name}", shape, dt))
        sem = lambda name: ctx.enter_context(nc.semaphore(f"ff_{name}"))
        ps = lambda name, shape: ctx.enter_context(nc.psum_tensor(f"ff_{name}", shape, F32))
        ident = sb("ident", [P, P])
        high = [sb(f"high_{n}", [P, CD * D if n == 0 else CD * F], F32R) for n in range(3)]
        b1 = sb("b1", [P, CF])
        bv = sb("bv", [P, CD])
        BO, G1, BE1, B2, G2, BE2 = range(6)
        cx = sb("cx", [P, TF, H, DK + 1])
        rl = sb("rl", [P, TF, H])
        xr = sb("xr", [P, TF, D])
        cT = [sb(f"cT_{n}", [P, CD, RF], F32R) for n in range(2)]
        hT = [sb(f"hT_{n}", [P, CD, RF], F32R) for n in range(2)]
        h1 = [sb(f"h1_{b}", [P, TF, D]) for b in range(2)]
        RING, LAG = 3, 2
        hid = [sb(f"hid_{n}", [P, RING, BANK], F32R) for n in range(2)]
        raw = [scratch[:, b * BANK:(b + 1) * BANK] for b in range(2)]
        CONTEXT, ATTN, NORM = 3, 4, 5
        SECOND = 0
        bn = sb("bn", [P, 2, TF, 6])
        mv = sb("mv", [P, 2, TF, 2])
        rs = sb("rs", [P, 2, TF, 1])
        eps = sb("eps", [P, 1])
        zero = sb("zero", [P, 1])
        tr_ps = ps("tr_ps", [P, 2, BANK])
        wo_ps = ps("wo_ps", [P, 2, D])
        w2_ps = ps("w2_ps", [P, 2, D])
        hid_ps = ps("hid_ps", [P, 2, BANK])
        c_in, cx_in, x_in, stored = sem("c_in"), sem("cx_in"), sem("x_in"), sem("stored")
        high_done, rest_done = sem("high_done"), sem("rest_done")
        tr_done = sem("tr_done")
        xh_done, xl_done = sem("xh_done"), sem("xl_done")
        wo_done, wo_read = sem("wo_done"), sem("wo_read")
        used = sem("used")
        w2_read = sem("w2_read")
        hid_done, relu_done = sem("hid_done"), sem("relu_done")
        hh_done, hl_done = sem("hh_done"), sem("hl_done")
        h1_done, ob_done = sem("h1_done"), sem("ob_done")
        var_done, root_done = sem("var_done"), sem("root_done")
        rl_done, cn_done = sem("rl_done"), sem("cn_done")
        chain = sem("chain")
        bn_done = sem("bn_done")
        added = sem("added")
        eps_set = sem("eps_set")
        passed = sem("passed")
        block = ctx.enter_context(nc.Block())
        first = lambda g: isinstance(g, int) and g == 0
        FB = BANK // RF
        HB1 = CF // FB
        TB = CD // FB
        SLICE = CD * D
        SLICES = [(n, s) for n in range(3) for s in range(1 if n == 0 else CD * F // SLICE)]
        ready = lambda n: max(i for i, (m, _) in enumerate(SLICES) if m == n) + 1

        def each_group(engine, step):
            with engine.Fori(0, NF // 2 - 1) as pair:
                for b in range(2):
                    step(pair * 2 + (1 + b), (1 + b) % 2)

        def tr_at(g, kind):
            return g * 2 * TB + kind * TB

        def norm_at(g, kind, t):
            if kind == 0:
                return t if first(g) else (g - 1) * (2 * TF) + (TF + t)
            last = isinstance(g, int) and g == NF - 1
            return g * (2 * TF) + ((TF if last else 2 * TF) + t)

        @block.sync
        def _(sp):
            rows = lambda ap, g: ap[bass.ds(g * RF, RF), :].rearrange("(t p) f -> p t f", p=P)

            def load_cx(g):
                if not first(g):
                    wait_alone(sp, passed, (cn_done, g))
                sp.dma_start(cx[:, :, :, :].rearrange("p t h d -> p t (h d)"), rows(ctx_rows, g)).then_inc(cx_in, 16)

            def load_x(g):
                if not first(g):
                    wait_alone(sp, passed, (h1_done, g * TF))
                sp.dma_start(xr[:, :, :], rows(x_rows, g)).then_inc(x_in, 16)

            def store(g, b):
                wait_alone(sp, passed, (ob_done, (g + 1) * TF))
                sp.dma_start(rows(out, g), h1[b][:, :, :]).then_inc(stored, 16)

            load_cx(0)
            load_x(0)
            sp.dma_start(ident[:, :], ident_in).then_inc(c_in, 16)
            sp.dma_start(bv[:, :], b_v).then_inc(c_in, 16)
            sp.dma_start(b1[:, :], b_1).then_inc(c_in, 16)

            def step(g, b):
                load_cx(g + 1)
                load_x(g + 1)
                if not first(g):
                    store(g - 1, 1 - b)

            step(0, 0)
            each_group(sp, step)
            store(NF - 2, 0)
            store(NF - 1, 1)
            sp.wait_ge(stored, 16 * NF)

        @block.tensor
        def _(pe):
            pe.wait_ge(c_in, 16 * 3)

            def transposes(g, kind, src):
                for n in range(TB):
                    at = tr_at(g, kind) + n
                    if not (first(g) and kind == 0):
                        pe.wait_ge(xl_done, at - 1)
                    for j in range(FB):
                        for t in range(TF):
                            c = n * FB + j
                            mm = pe.transpose(tr_ps[:, n % 2, (j * TF + t) * P:(j * TF + t + 1) * P],
                                              src[:, t, c * P:(c + 1) * P], ident[:, :])
                    mm.then_inc(tr_done, 1)

            PASSES = ((0, 0), (1, 0), (0, 1))

            def part(n, k):
                return (high, rest)[k][n].rearrange("p (c o) -> p c o", c=CD if n < 2 else CF)

            def context(g, b):
                pe.wait_ge(cn_done, g + 1)
                transposes(g, 0, h1[b])

            def attn_rows(g):
                pe.wait_ge(xl_done, tr_at(g, 1))
                if first(g):
                    pe.wait_ge(rest_done, ready(0))
                for t in range(TF):
                    if not first(g):
                        pe.wait_ge(wo_read, g * TF + t - 1)
                    todo = [(i, l, k) for i in range(CD) for l, k in PASSES]
                    for i, l, k in todo:
                        mm = pe.matmul(wo_ps[:, t % 2, :], cT[l][:, i, t * P:(t + 1) * P], part(0, k)[:, i, :],
                                       start=(i, l, k) == todo[0], stop=(i, l, k) == todo[-1])
                    mm.then_inc(wo_done, 1)

            def hidden_rows(g, b):
                pe.wait_ge(h1_done, (g + 1) * TF)
                transposes(g, 1, h1[b])

            def hidden(g, n):
                if not (first(g) and n < 2):
                    pe.wait_ge(relu_done, g * HB1 + n - 1)
                todo = [(i, l, k) for i in range(CD) for l, k in PASSES]
                for j in range(FB):
                    f = n * FB + j
                    for i, l, k in todo:
                        mm = pe.matmul(hid_ps[:, n % 2, j * RF:(j + 1) * RF], part(1, k)[:, i, f * P:(f + 1) * P], hT[l][:, i, :],
                                       start=(i, l, k) == todo[0], stop=(i, l, k) == todo[-1])
                mm.then_inc(hid_done, 1)

            def out_rows(g, n):
                pe.wait_ge(hl_done, g * HB1 + n + 1)
                if first(g):
                    pe.wait_ge(rest_done, ready(1) + n // 2 + 1)
                for t in range(TF):
                    if n == 0 and not first(g):
                        pe.wait_ge(w2_read, (g - 1) * TF + t + 1)
                    for j in range(FB):
                        for l, k in PASSES:
                            start = n == 0 and j == 0 and (l, k) == PASSES[0]
                            stop = n == HB1 - 1 and j == FB - 1 and (l, k) == PASSES[-1]
                            mm = pe.matmul(w2_ps[:, t, :], hid[l][:, n % RING, j * RF + t * P:j * RF + (t + 1) * P],
                                           part(2, k)[:, n * FB + j, :], start=start, stop=stop)
                mm.then_inc(used, 1)

            def step(g, b):
                pe.wait_ge(xl_done, tr_at(g + 1, 0))
                if first(g):
                    pe.wait_ge(rest_done, ready(1))
                more = not (isinstance(g, int) and g == NF - 1)
                for n in range(HB1 + LAG):
                    if n < HB1:
                        hidden(g, n)
                    if n == HB1 + LAG - 1 and more:
                        hidden_rows(g + 1, 1 - b)
                    if n >= LAG:
                        out_rows(g, n - LAG)
                    if n == CONTEXT and more:
                        context(g + 1, 1 - b)
                    if n == ATTN and more:
                        attn_rows(g + 1)

            context(0, 0)
            attn_rows(0)
            hidden_rows(0, 0)
            step(0, 0)
            each_group(pe, step)
            step(NF - 1, 1)

        @block.scalar
        def _(act):
            act.wait_ge(c_in, 16 * 3)
            act.wait_ge(eps_set, 2)

            def split(i):
                n, s = SLICES[i]
                act.activation(high[n][:, s * SLICE:(s + 1) * SLICE], weights[n][:, s * SLICE:(s + 1) * SLICE], ACT.Copy)\
                   .then_inc(high_done, 1)

            assert HB1 == 2 * (len(SLICES) - ready(1))

            def transposed(g, kind):
                for n in range(TB):
                    act.wait_ge(tr_done, tr_at(g, kind) + n + 1)
                    for j in range(FB):
                        c = n * FB + j
                        bias = bv[:, c:c + 1] if kind == 0 else zero[:, :]
                        ins = act.activation((cT, hT)[kind][0][:, c, :], tr_ps[:, n % 2, j * RF:(j + 1) * RF], ACT.Identity, bias=bias)
                    ins.then_inc(xh_done, 1)

            def root(g, kind, t):
                act.wait_ge(var_done, norm_at(g, kind, t) + 1)
                act.activation(rs[:, kind, t, :], mv[:, kind, t, 1:2], ACT.Sqrt, bias=eps[:, :]).then_inc(root_done, 1)

            def hidden(g, n):
                act.wait_ge(hid_done, g * HB1 + n + 1)
                if not (first(g) and n < RING):
                    act.wait_ge(used, g * HB1 + n - RING + 1)
                if not (first(g) and n < 2):
                    act.wait_ge(hl_done, g * HB1 + n - 1)
                for j in range(FB):
                    f, cols = n * FB + j, slice(j * RF, (j + 1) * RF)
                    ins = act.activation(raw[n % 2][:, cols], hid_ps[:, n % 2, cols], ACT.Relu, bias=b1[:, f:f + 1])
                ins.then_inc(relu_done, 1)
                act.wait_ge(relu_done, g * HB1 + n + 1)
                act.activation(hid[0][:, n % RING, :], raw[n % 2], ACT.Copy).then_inc(hh_done, 1)

            def step(g, b=None):
                transposed(g, 1)
                more = not (isinstance(g, int) and g == NF - 1)
                for n in range(HB1):
                    if n % 2 == 0 and first(g):
                        split(ready(1) + n // 2)
                    hidden(g, n)
                    if n == SECOND and not first(g):
                        for t in range(TF):
                            root(g - 1, 1, t)
                    if n == CONTEXT and more:
                        transposed(g + 1, 0)
                    if n == NORM + 1 and more:
                        for t in range(TF):
                            root(g + 1, 0, t)

            split(0)
            transposed(0, 0)
            for i in range(1, ready(1)):
                split(i)
            for t in range(TF):
                root(0, 0, t)
            step(0)
            each_group(act, step)
            step(NF - 1)
            for t in range(TF):
                root(NF - 1, 1, t)

        @block.vector
        def _(dve):
            dve.memset(eps[:, :], EPS).then_inc(eps_set, 1)
            dve.memset(zero[:, :], 0.0).then_inc(eps_set, 1)
            dve.wait_ge(c_in, 16 * 3)
            CH = 3

            def split(i):
                n, s = SLICES[i]
                cols = slice(s * SLICE, (s + 1) * SLICE)
                dve.wait_ge(high_done, i + 1)
                dve.tensor_tensor(rest[n][:, cols], weights[n][:, cols], high[n][:, cols].bitcast(F32), ALU.subtract)\
                   .then_inc(rest_done, 1)

            def divide(g, b):
                cn = h1[b]
                dve.wait_ge(cx_in, g * 16 + 16)
                dve.reciprocal(rl[:, :, :], cx[:, :, :, DK]).then_inc(rl_done, 1)
                dve.wait_ge(rl_done, g + 1)
                if not (isinstance(g, int) and g < 2):
                    dve.wait_ge(stored, (g - 1) * 16)
                for t in range(TF):
                    ins = dve.tensor_tensor(cn[:, t, :].rearrange("p (h d) -> p h d", d=DK), cx[:, t, :, 0:DK],
                                            rl[:, t, :].unsqueeze(2).broadcast_to([P, H, DK]), ALU.mult)
                ins.then_inc(cn_done, 1)

            def transposed(g, kind):
                xT = (cT, hT)[kind]
                for n in range(TB):
                    dve.wait_ge(xh_done, tr_at(g, kind) + n + 1)
                    for j in range(FB):
                        c = n * FB + j
                        bias = bv[:, c:c + 1] if kind == 0 else 0.0
                        ins = dve.scalar_tensor_tensor(xT[1][:, c, :], tr_ps[:, n % 2, j * RF:(j + 1) * RF], bias,
                                                       xT[0][:, c, :].bitcast(F32), op0=ALU.add, op1=ALU.subtract)
                    ins.then_inc(xl_done, 1)

            def add_sums(g, kind, t, b):
                rows = (xr, h1[b])[kind][:, t, :]
                dve.tensor_tensor(rows, rows, vec[:, (BO, B2)[kind], :], ALU.add).then_inc(added, 1)
                dve.wait_ge(added, norm_at(g, kind, t) + 1)
                if kind == 0:
                    dve.wait_ge(wo_done, g * TF + t + 1)
                else:
                    dve.wait_ge(used, (g + 1) * HB1)
                dve.tensor_tensor(rows, rows, (wo_ps, w2_ps)[kind][:, t, :], ALU.add).then_inc((wo_read, w2_read)[kind], 1)

            def stats(g, kind, t, b):
                add_sums(g, kind, t, b)
                dve.wait_ge((wo_read, w2_read)[kind], g * TF + t + 1)
                dve.bn_stats(bn[:, kind, t, :], (xr, h1[b])[kind][:, t, :]).then_inc(bn_done, 1)
                wait_alone(dve, passed, (bn_done, norm_at(g, kind, t) + 1))
                dve.bn_aggr(mv[:, kind, t, :], bn[:, kind, t, :]).then_inc(var_done, 1)

            def norm(g, kind, t, b):
                rows, gain, shift, done = ((xr, G1, BE1, h1_done), (h1[b], G2, BE2, ob_done))[kind]
                rows = rows[:, t, :]
                at = norm_at(g, kind, t) * CH

                def link(ins):
                    nonlocal at
                    at = at + 1
                    ins.then_inc(chain, 1)
                    dve.wait_ge(chain, at)
                dve.wait_ge(root_done, norm_at(g, kind, t) + 1)
                link(dve.reciprocal(rs[:, kind, t, :], rs[:, kind, t, :]))
                link(dve.tensor_scalar(rows, rows, mv[:, kind, t, 0:1], rs[:, kind, t, :], op0=ALU.subtract, op1=ALU.mult))
                link(dve.tensor_tensor(rows, rows, vec[:, gain, :], ALU.mult))
                dve.tensor_tensor(h1[b][:, t, :], rows, vec[:, shift, :], ALU.add).then_inc(done, 1)
                dve.wait_ge(done, g * TF + t + 1)

            def attn_stats(g, b):
                dve.wait_ge(x_in, g * 16 + 16)
                for t in range(TF):
                    stats(g, 0, t, b)

            def hidden(g, n):
                dve.wait_ge(hh_done, g * HB1 + n + 1)
                dve.tensor_tensor(hid[1][:, n % RING, :], raw[n % 2], hid[0][:, n % RING, :].bitcast(F32),
                                  ALU.subtract).then_inc(hl_done, 1)

            def step(g, b):
                transposed(g, 1)
                more = not (isinstance(g, int) and g == NF - 1)
                for n in range(HB1):
                    if n % 2 == 0 and first(g):
                        split(ready(1) + n // 2)
                    if n == SECOND and not first(g):
                        for t in range(TF):
                            stats(g - 1, 1, t, 1 - b)
                    hidden(g, n)
                    if SECOND <= n < SECOND + TF and not first(g):
                        norm(g - 1, 1, n - SECOND, 1 - b)
                    if n == CONTEXT - 1 and more:
                        divide(g + 1, 1 - b)
                    if n == CONTEXT and more:
                        transposed(g + 1, 0)
                    if n == NORM and more:
                        attn_stats(g + 1, 1 - b)
                    if NORM < n <= NORM + TF and more:
                        if n == NORM + 1:
                            dve.wait_ge(tr_done, tr_at(g + 1, 1))
                        norm(g + 1, 0, n - NORM - 1, 1 - b)

            split(0)
            divide(0, 0)
            transposed(0, 0)
            for i in range(1, ready(1)):
                split(i)
            attn_stats(0, 0)
            dve.wait_ge(tr_done, tr_at(0, 1))
            for t in range(TF):
                norm(0, 0, t, 0)
            step(0, 0)
            each_group(dve, step)
            step(NF - 1, 1)
            for t in range(TF):
                stats(NF - 1, 1, t, 1)
            for t in range(TF):
                norm(NF - 1, 1, t, 1)


def layer(nc, a):
    dram = lambda name, shape, dt=F32: nc.dram_tensor(name, shape, dt, kind="Internal").ap()
    q_tab = dram("q_tab", [N, D])
    kv_tab = dram("kv_tab", [N, 2 * D])
    rec_tab = dram("rec_tab", [T * REC_TILE + P, REC], I32)
    ctx_rows = dram("ctx_rows", [N, H * (DK + 1)])
    with ExitStack() as ctx:
        sb = lambda name, shape, dt: ctx.enter_context(nc.sbuf_tensor(name, shape, dt))
        it_index = sb("it_index", [P, 2, IMAX], I32)
        it_reset = sb("it_reset", [P, IMAX], F32)
        rounds = sb("rounds", [P, 2], I32)
        project_and_list(nc, a, q_tab, kv_tab, rec_tab, it_index, it_reset, rounds)
        sizes = (("woT", CD, CD * D), ("w1T", CD, CD * F), ("w2T", CF, CF * D))
        vec = sb("vec", [P, 6, D], F32)
        with ExitStack() as loaded:
            w = [loaded.enter_context(nc.sbuf_tensor(f"w_{name}", [P, cols], F32)) for name, _, cols in sizes]
            early = [(raw[:, :].rearrange("p (c o) -> p c o", c=c), a[name].rearrange("(c p) o -> p c o", p=P))
                     for raw, (name, c, _) in zip(w, sizes)]
            early += [(vec[:, n, :], a[name].rearrange("(a o) -> a o", a=1).broadcast_to([P, D]))
                      for n, name in enumerate(("bo", "g1", "be1", "b2", "g2", "be2"))]
            attend(nc, early, a["adj_tab"], q_tab, kv_tab, rec_tab, it_index, it_reset, rounds, a["bk"], ctx_rows,
                   a["ident"], a["iota"])
        rest = [sb(f"rest_{name}", [P, cols], F32R) for name, _, cols in sizes]
        scratch = it_index[:, :, :].rearrange("p n i -> p (n i)").bitcast(F32)
        feed_forward(nc, a["x"], ctx_rows, w, rest, vec, scratch, a["bv"], a["b1"], a["ident"], a["out"])


def constants():
    p = np.arange(P)
    t = np.arange(T)
    own = p[:, None] * B // P == t[None, :]
    return {
        "ident": np.eye(P, dtype=np.float32),
        "iota": np.tile(np.arange(P, dtype=np.float32), (P, 1)),
        "iota_item": np.tile(np.arange(IMAX, dtype=np.float32), (P, 1)),
        "below": (p[:, None] < p[None, :]).astype(np.float32),
        "own": own.astype(np.float32),
        "column": p[:, None].astype(np.float32),
        "slot": np.arange(N).reshape(HI, LO).astype(np.float32),
        "number": (np.arange(N) - N // 2).reshape(P, B).astype(np.float16),
        "tile_c": np.tile(np.stack([t * N - 1, T * N - t * N + 1, -1 - t * P]).astype(np.float32), (HI, 1, 1)),
    }


def kernel(**inputs):
    import concourse.bacc as bacc
    from concourse.bass_utils import run_bass_kernel_spmd
    from concourse import mybir as _mybir

    given = {k.removeprefix("L0_gnn_"): np.asarray(v) for k, v in inputs.items()}
    names = {"bq": "bq", "bk": "bk", "bv": "bv", "bo": "bo", "b1": "b1", "b2": "b2",
             "g1": "ln1_g", "be1": "ln1_b", "g2": "ln2_g", "be2": "ln2_b"}
    arrays = {k: np.ascontiguousarray(given[v]) for k, v in names.items()}
    for k, v in {"wqT": "Wq", "wkT": "Wk", "wvT": "Wv", "woT": "Wo", "w1T": "W1", "w2T": "W2", "xT": "x"}.items():
        arrays[k] = np.ascontiguousarray(given[v].T)
    for k in ("bq", "bk", "bv", "b1"):
        arrays[k] = np.ascontiguousarray(arrays[k].reshape(-1, P).T)
    arrays["x"] = np.ascontiguousarray(given["x"])
    adj = given["adj"].reshape(T, P, N).transpose(0, 2, 1).reshape(T * N, P)
    arrays["adj_tab"] = np.concatenate([adj, np.zeros((1, P), adj.dtype)])
    arrays |= constants()

    nc = bacc.Bacc("TRN2", target_bir_lowering=False, num_devices=1)
    args = {k: nc.dram_tensor(f"in_{k}", v.shape, _mybir.dt.from_np(v.dtype), kind="ExternalInput").ap()
            for k, v in arrays.items()}
    args["out"] = nc.dram_tensor("out_rows", [N, D], F32, kind="ExternalOutput").ap()
    layer(nc, args)
    r = run_bass_kernel_spmd(nc, [{f"in_{k}": v for k, v in arrays.items()}], core_ids=[0])
    return r.results[0]["out_rows"]
```
